# Optimizing a Trainium2 kernel written in Bass

```python
import numpy as np
import jax
import jax.numpy as jnp

def _softmax(x, axis=-1):
    return jax.nn.softmax(x, axis=axis)

def _gelu(x):
    return jax.nn.gelu(x, approximate=True)

def _silu(x):
    return jax.nn.silu(x)

def _sigmoid(x):
    return jax.nn.sigmoid(x)

def _layernorm(x, axis=-1, eps=1e-05):
    m = jnp.mean(x, axis=axis, keepdims=True)
    v = jnp.var(x, axis=axis, keepdims=True)
    return (x - m) / jnp.sqrt(v + eps)

def _scatter_add(tgt, idx, src, axis=0):
    return tgt.at[idx].add(src)

def _segment_sum(src, seg, n):
    return jax.ops.segment_sum(src, seg, n)
kernel_name = 'mk_xattn_ffn_d1_seqx_r8_d88444'

def setup_inputs(seed: int=0):
    np.random.seed(seed)
    _w = jnp.asarray

    def _rec_inputs():
        import jax
        import jax.numpy as jnp
        _rk = jax.random.key(seed)
        x = -0.0002928 + 1 * jax.random.normal(jax.random.fold_in(_rk, 1), (4, 256, 128), jnp.float32)
        _lenS = 256 - jax.random.randint(jax.random.fold_in(_rk, 7), (4,), 0, max(1, 256 // 4) + 1, jnp.int32)
        _lenS2 = 1601 - jax.random.randint(jax.random.fold_in(_rk, 8), (4,), 0, max(1, 1601 // 4) + 1, jnp.int32)
        _ctx_1024P = jax.random.normal(jax.random.fold_in(_rk, 11), (4, 16, 128), jnp.float32)
        _ctx_1024c = jax.random.dirichlet(jax.random.fold_in(_rk, 511), 0.3 * jnp.ones((16,), jnp.float32), (4, 1601))
        _ctx_1024t = jnp.einsum('bsk,bkd->bsd', _ctx_1024c, _ctx_1024P)
        _ctx_1024t = _ctx_1024t * jax.lax.rsqrt(jnp.mean(jnp.square(_ctx_1024t)) + 1e-12) * 0.953939
        ctx_1024 = -1.39393e-06 + 0.999914 * (_ctx_1024t + 0.3 * jax.random.normal(jax.random.fold_in(_rk, 611), (4, 1601, 128), jnp.float32))
        _validS = jnp.arange(256)[None, :] < _lenS[:, None]
        _validS2 = jnp.arange(1601)[None, :] < _lenS2[:, None]
        _causal = jnp.tril(jnp.ones((256, 256), dtype=bool))
        mask_Bx1xSxS2_ff0 = jnp.where(jnp.ones((4, 1, 256, 1601), dtype=bool), 0.0, -1000000000.0).astype(jnp.float32)
        return (x, ctx_1024, mask_Bx1xSxS2_ff0)
    x, ctx_1024, mask_Bx1xSxS2_ff0 = _rec_inputs()

    def _L0_xattn_setup():
        import jax, jax.numpy as jnp
        import numpy as np
        B, S, D, H = (2, 256, 128, 16)
        HD = D // H

        def _split_heads(x):
            b, s, _ = x.shape
            return x.reshape(b, s, H, HD).transpose(0, 2, 1, 3)
        key = jax.random.key(seed)
        ks = jax.random.split(key, 12)
        init = lambda k, shape: jax.random.normal(k, shape, dtype=jnp.float32) * (1.0 / np.sqrt(shape[0]))
        return {'q': jax.random.normal(ks[0], (B, S, D), dtype=jnp.float32), 'k': jax.random.normal(ks[1], (B, S, D), dtype=jnp.float32), 'v': jax.random.normal(ks[2], (B, S, D), dtype=jnp.float32), 'mask': jnp.zeros((B, 1, S, S), dtype=jnp.float32), 'Wq': init(ks[3], (D, D)), 'bq': jnp.zeros((D,), jnp.float32), 'Wk': init(ks[4], (D, D)), 'bk': jnp.zeros((D,), jnp.float32), 'Wv': init(ks[5], (D, D)), 'bv': jnp.zeros((D,), jnp.float32), 'Wo': init(ks[6], (D, D)), 'bo': jnp.zeros((D,), jnp.float32)}
    _L0_xattn_all = _L0_xattn_setup()
    _L0_xattn_in = {k: v for k, v in _L0_xattn_all.items() if k in ('Wq', 'bq', 'Wk', 'bk', 'Wv', 'bv', 'Wo', 'bo')}
    del _L0_xattn_all

    def _L0_ffn_setup():
        import jax, jax.numpy as jnp
        import numpy as np
        EPS = 1e-12

        def _l2norm(v):
            n = jnp.sqrt(jnp.sum(v * v, axis=-1, keepdims=True))
            return v / jnp.maximum(n, EPS)
        key = jax.random.key(seed)
        ks = jax.random.split(key, 6)
        B, S, D, F, E = (2, 256, 128, 512, 8)
        std = 0.02
        return {'x': jax.random.normal(ks[0], (B, S, D), jnp.float32), 'Wp': jax.random.normal(ks[1], (D, D), jnp.float32) * (1.0 / np.sqrt(D)), 'sim_matrix': jax.random.normal(ks[2], (E, D), jnp.float32) * std, 'temperature': jnp.asarray(1.0, jnp.float32), 'W1': jax.random.normal(ks[3], (E, D, F), jnp.float32) * (1.0 / np.sqrt(D)), 'b1': jnp.zeros((E, F), jnp.float32), 'W2': jax.random.normal(ks[4], (E, F, D), jnp.float32) * (1.0 / np.sqrt(F)), 'b2': jnp.zeros((E, D), jnp.float32)}
    _L0_ffn_all = _L0_ffn_setup()
    _L0_ffn_in = {k: v for k, v in _L0_ffn_all.items() if k in ('Wp', 'sim_matrix', 'temperature', 'W1', 'b1', 'W2', 'b2')}
    del _L0_ffn_all
    return {'x': x, 'ctx_1024': ctx_1024, 'mask_Bx1xSxS2_ff0': mask_Bx1xSxS2_ff0, 'L0_xattn_Wq': _L0_xattn_in['Wq'], 'L0_xattn_bq': _L0_xattn_in['bq'], 'L0_xattn_Wk': _L0_xattn_in['Wk'], 'L0_xattn_bk': _L0_xattn_in['bk'], 'L0_xattn_Wv': _L0_xattn_in['Wv'], 'L0_xattn_bv': _L0_xattn_in['bv'], 'L0_xattn_Wo': _L0_xattn_in['Wo'], 'L0_xattn_bo': _L0_xattn_in['bo'], 'L0_ffn_Wp': _L0_ffn_in['Wp'], 'L0_ffn_sim_matrix': _L0_ffn_in['sim_matrix'], 'L0_ffn_temperature': _L0_ffn_in['temperature'], 'L0_ffn_W1': _L0_ffn_in['W1'], 'L0_ffn_b1': _L0_ffn_in['b1'], 'L0_ffn_W2': _L0_ffn_in['W2'], 'L0_ffn_b2': _L0_ffn_in['b2']}

def reference(x, ctx_1024, mask_Bx1xSxS2_ff0, L0_xattn_Wq, L0_xattn_bq, L0_xattn_Wk, L0_xattn_bk, L0_xattn_Wv, L0_xattn_bv, L0_xattn_Wo, L0_xattn_bo, L0_ffn_Wp, L0_ffn_sim_matrix, L0_ffn_temperature, L0_ffn_W1, L0_ffn_b1, L0_ffn_W2, L0_ffn_b2):
    import jax
    import jax.numpy as jnp

    def _L0_xattn_ref(q, k, v, mask, Wq, bq, Wk, bk, Wv, bv, Wo, bo):
        import jax, jax.numpy as jnp
        import numpy as np
        B, S, D, H = (2, 256, 128, 16)
        HD = D // H

        def _split_heads(x):
            b, s, _ = x.shape
            return x.reshape(b, s, H, HD).transpose(0, 2, 1, 3)
        qh = _split_heads(q @ Wq + bq)
        kh = _split_heads(k @ Wk + bk)
        vh = _split_heads(v @ Wv + bv)
        scores = jnp.einsum('bhqd,bhkd->bhqk', qh, kh) / jnp.sqrt(jnp.float32(D))
        scores = scores + mask * -1000000000.0
        attn = jax.nn.softmax(scores, axis=-1)
        out = jnp.einsum('bhqk,bhkd->bhqd', attn, vh)
        out = out.transpose(0, 2, 1, 3).reshape(q.shape[0], -1, D)
        return out @ Wo + bo

    def _L0_ffn_ref(x, Wp, sim_matrix, temperature, W1, b1, W2, b2):
        import jax, jax.numpy as jnp
        import numpy as np
        EPS = 1e-12

        def _l2norm(v):
            n = jnp.sqrt(jnp.sum(v * v, axis=-1, keepdims=True))
            return v / jnp.maximum(n, EPS)
        E = sim_matrix.shape[0]
        top_k = 2
        proj = jnp.einsum('bsd,ed->bse', x, Wp)
        pn = _l2norm(proj)
        sn = _l2norm(sim_matrix)
        gate_scores = jnp.einsum('bsd,ed->bse', pn, sn) / temperature
        top_v, top_i = jax.lax.top_k(gate_scores, top_k)
        gate_probs = jax.nn.softmax(top_v, axis=-1)
        comb = jnp.sum(jax.nn.one_hot(top_i, E, dtype=x.dtype) * gate_probs[..., None], axis=-2)
        h = jax.nn.gelu(jnp.einsum('bsd,edf->ebsf', x, W1) + b1[:, None, None, :], approximate=False)
        eo = jnp.einsum('ebsf,efd->ebsd', h, W2) + b2[:, None, None, :]
        out = jnp.einsum('ebsd,bse->bsd', eo, comb)
        return out
    x = x + _L0_xattn_ref(_layernorm(x, axis=-1), ctx_1024, ctx_1024, mask_Bx1xSxS2_ff0, L0_xattn_Wq, L0_xattn_bq, L0_xattn_Wk, L0_xattn_bk, L0_xattn_Wv, L0_xattn_bv, L0_xattn_Wo, L0_xattn_bo)
    x = x + _L0_ffn_ref(_layernorm(x, axis=-1), L0_ffn_Wp, L0_ffn_sim_matrix, L0_ffn_temperature, L0_ffn_W1, L0_ffn_b1, L0_ffn_W2, L0_ffn_b2)
    return x

_drawn_inputs = setup_inputs


def setup_inputs(seed=0):
    import zlib

    import numpy as np

    out = dict(_drawn_inputs(seed))
    spreads = {'L0_xattn_bq': (0.0, 0.1),
     'L0_xattn_bk': (0.0, 0.1),
     'L0_xattn_bv': (0.0, 0.1),
     'L0_xattn_bo': (0.0, 0.1),
     'L0_ffn_b1': (0.0, 0.1),
     'L0_ffn_b2': (0.0, 0.1)}
    factors = {}
    for name, (base, spread) in spreads.items():
        noise = np.random.default_rng([zlib.crc32(name.encode()), seed]).standard_normal(out[name].shape)
        drawn = base * np.exp(spread * noise) if base else spread * noise
        out[name] = jnp.asarray(drawn.astype(out[name].dtype))
    for name, factor in factors.items():
        out[name] = (out[name] * factor).astype(out[name].dtype)
    return out
```

```python
from contextlib import ExitStack

import concourse.bass as bass
from concourse import mybir

ALU = mybir.AluOpType
ACT = mybir.ActivationFunctionType
AX_X = mybir.AxisListType.X
F32 = mybir.dt.float32
BF16 = mybir.dt.bfloat16
U32 = mybir.dt.uint32

P = 128
LN_EPS = 1e-5
L2_EPS = 1e-12
MASK_SCALE = -1e9
SUM_FLOOR = 1e-36
SUM_LEAST, SUM_MOST = 1e-25, 1e30
PARTS = 3
TERMS = [(0, 0), (0, 1), (0, 2), (1, 0), (1, 1), (2, 0)]
LAG = 2


def layer(nc, x, ctx_kv, mask, Wq, bq, Wk, bk, Wv, bv, Wo, bo, Wp, sim, temp, W1, b1, W2, b2, out):
    B, S, D = x.shape
    KV = ctx_kv.shape[1]
    E, _, F = W1.shape
    H = 16
    HD = D // H
    HG = 4
    PAIRS = H // 2
    PR = 2 * HD
    CROW = len(TERMS) * PR
    KROWS = CROW + PARTS
    NCH = -(-KV // P)
    KEYS = [min(P, KV - c * P) for c in range(NCH)]
    SLOTS = HG * NCH
    TT = S // P
    NT = B * TT
    FC = F // P
    EF = E * FC
    GW = D + E
    INV_SQRT_D = float(D) ** -0.5
    BANK = 512
    NK4 = -(-NCH // 4)
    NM2 = -(-NCH // 2)
    MB = 3

    before = [("bias", 0, 0)] + [("ctxT", 0, i) for i in range(NK4)] + [("kT", 0, i) for i in range(NK4)] + \
        [("xnT0", 0, i) for i in range(NT // 4)] + [("q", 0, i) for i in range(B * S // BANK)] + \
        [("shift", 0, 0)] + [("v", 0, i) for i in range(NK4)] + [("maskT", 0, i) for i in range(MB)]
    first_batch = [(i, "maskT", 0, MB + i) for i in range(NM2 - MB)] + \
        [(27, "simT", 0, 0), (29, "WpT", 0, 0), (32, "WpSim", 0, 0)]
    during = [(0, "maskT", 0, 5), (1, "v", 0, 2), (2, "maskT", 0, 6), (3, "v", 0, 3), (4, "oT", -1, 3), (5, "ctxT", 1, 0), (6, "onT", -1, 0),
              (7, "ctxT", 1, 1), (8, "wo", -1, 0), (9, "ctxT", 1, 2), (10, "ctxT", 1, 3), (11, "xnT", -1, 0),
              (12, "kT", 1, 0), (13, "gate", -1, 0), (14, "kT", 1, 1), (15, "kT", 1, 2), (16, "kT", 1, 3),
              (17, "combT", -1, 0), (18, "oT", 0, 0), (19, "b2", -1, 0), (24, "shift", 1, 0), (31, "oT", 0, 1),
              (42, "maskT", 1, 0), (43, "oT", 0, 2), (44, "maskT", 1, 1), (46, "maskT", 1, 2),
              (47, "v", 1, 0), (48, "maskT", 1, 3), (50, "maskT", 1, 4), (51, "v", 1, 1)]
    after = [("oT", B - 1, 3), ("verdict", 0, 0), ("onT", B - 1, 0), ("wo", B - 1, 0), ("xnT", B - 1, 0), ("gate", B - 1, 0),
             ("combT", B - 1, 0), ("b2", B - 1, 0)]
    BY_SCALAR = ("ctxT", "kT", "maskT", "onT")
    HALF = E // 2
    UPS = HALF * FC // 2
    DOWNS = HALF * TT
    BURST = [20, 36]
    DOWN = [21, 37]

    with ExitStack() as ctx:
        def sb(name, shape, dt=F32):
            return ctx.enter_context(nc.sbuf_tensor(name, shape, dt))

        def psum(name, shape):
            return ctx.enter_context(nc.psum_tensor(name, shape, F32))

        xs = sb("xs", [P, NT, D])
        ctx_nat = sb("ctx_nat", [P, NCH, D])
        mask_nat = sb("mask_nat", [P, MB, TT, 2 * P])
        maskT = sb("maskT", [P, NCH, S])
        ctxT = sb("ctxT", [P, KV])
        kT = sb("kT", [P, KV])
        kpart = [sb(f"kpart{i}", [P, KV], BF16) for i in range(PARTS)]
        kstack_flat = sb("kstack", [KROWS, PAIRS * KV], BF16)
        kstack = kstack_flat[:, :].rearrange("r (p k) -> r p k", p=PAIRS)
        qstack = sb("qstack", [KROWS, B, PAIRS, 2, S], BF16)
        vals = sb("vals", [P, NCH, H, HD + 1])
        masked = sb("masked", [P, 2, 4 * S])
        probs = sb("probs", [P, 2, 4 * S])
        w1 = sb("w1", [P, E, F])
        w2 = sb("w2", [P, EF, D])
        wq, wk, wv, wp = (sb(n, [P, D]) for n in ("wq", "wk", "wv", "wp"))
        wo = sb("wo", [P, D])
        bv_all, bo_all = sb("bv_all", [P, D]), sb("bo_all", [P, D])
        bias_rows = sb("bias_rows", [EF + 2, D])
        bias_cols = sb("bias_cols", [P, EF + 2])
        b2_rows = sb("b2_rows", [E, D])
        sim_rows = sb("sim_rows", [E, D])
        simT = sb("simT", [P, E])
        tiny = sb("tiny", [P, 16])
        wg = sb("wg", [P, GW])
        ident = sb("ident", [P, P])
        blk = sb("blk", [P, H])
        negblk = sb("negblk", [P, H])
        half = sb("half", [P, 2])
        minus_half = sb("minus_half", [P, NT])
        iota8 = sb("iota8", [P, E])
        stats = sb("stats", [P, NT, 6])
        moments = sb("moments", [P, NT, 2])
        var_eps = sb("var_eps", [P, NT])
        rstd = sb("rstd", [P, NT])
        qs = sb("qs", [P, B * S])
        kmax = sb("kmax", [P, 1])
        ub = sb("ub", [P, S])
        shift = sb("shift", [H, S])
        shift_part = [sb(f"shift_part{i}", [H, S], BF16) for i in range(PARTS)]
        osum = sb("osum", [P, S])
        onat = sb("onat", [P, TT, H, HD])
        onT = sb("onT", [P, S])
        xn2 = sb("xn2", [P, TT, D])
        xn2T = sb("xn2T", [P, S])
        graw = sb("graw", [P, TT, E])
        gsc = sb("gsc", [P, TT, E])
        sumsq = sb("sumsq", [P, TT])
        rnorm = sb("rnorm", [P, TT])
        junk = sb("junk", [P, D])
        top = sb("top", [P, TT, 8])
        topi = sb("topi", [P, TT, 8], U32)
        topf = sb("topf", [P, TT, 8])
        diff = sb("diff", [P, TT])
        ediff = sb("ediff", [P, TT])
        den = sb("den", [P, TT])
        p1, p2 = sb("p1", [P, TT]), sb("p2", [P, TT])
        comb = sb("comb", [P, TT, E])
        hot = sb("hot", [P, E])
        combT = sb("combT", [E, S])
        inverses = sb("inverses", [P, B * HG, TT, 4])
        fine = sb("fine", [P, 2])
        verdict = sb("verdict", [1, 4], mybir.dt.int32)
        top_score = sb("top_score", [P, 2, 8])
        top_rows = sb("top_rows", [P, 4 * S])
        hid = sb("hid", [P, HALF * FC, S])
        flat = hid[:, :, :].rearrange("p a s -> p (a s)")
        xn1 = flat[:, 0:NT * D]
        xn1T = flat[:, NT * D:NT * D + B * S]
        qrest = xn1
        flat16 = flat.bitcast(BF16)
        qpart = [flat16[:, (4 + i) * B * S:(5 + i) * B * S] for i in range(PARTS)]
        w2_16 = w2[:, :, :].rearrange("p a d -> p (a d)").bitcast(BF16)
        qhalf = [w2_16[:, 2 * i * B * S:2 * (i + 1) * B * S].rearrange("p (b a s) -> p b a s", b=B, a=2)
                 for i in range(PARTS)]

        score = [psum(f"score{i}", [P, 4 * S]) for i in range(2)]
        pv = psum("pv", [P, BANK])
        misc = psum("misc", [P, BANK])
        ffn = [psum(f"ffn{i}", [P, BANK]) for i in range(2)]
        free = [misc, ffn[0], ffn[1]] + [score[i][:, j * BANK:(j + 1) * BANK] for i in range(2) for j in range(2)]

        def bank_of(n):
            return free[n % len(free)] if n < len(before) else misc

        def used_before(n):
            if n < len(before):
                return n - len(free) if n >= len(free) else None
            return n - 1

        def attempt(ctx, exact):
            steps = list(before)
            at_slot = {(b, slot): [] for b in range(B) for slot in range(SLOTS)}
            for b in range(B):
                own = {(kind, b + rel, part) for _, kind, rel, part in first_batch} if b == 0 else set()
                planned = (first_batch if b == 0 else []) + [s for s in during if (s[1], b + s[2], s[3]) not in own]
                if exact:
                    planned = [(0 if s[1] == "maskT" and s[2] == 0 else s[0],) + s[1:] for s in planned]
                for slot, kind, rel, part in sorted(planned):
                    if 0 <= b + rel < B and (kind, b + rel, part) not in before:
                        at_slot[b, slot].append((len(steps), kind, b + rel, part))
                        steps.append((kind, b + rel, part))
            first_after = len(steps)
            steps += after
            number = {s: n for n, s in enumerate(steps)}
            by_scalar = [sum(k in BY_SCALAR for k, _, _ in steps[:n + 1]) for n in range(len(steps))]
            by_vector = [n + 1 - by_scalar[n] for n in range(len(steps))]

            def sem(name):
                return ctx.enter_context(nc.semaphore(name + ("_exact" if exact else "")))

            x_in, w_in, ctx_in, w1_in, w2_in = (sem(n) for n in ("x_in", "w_in", "ctx_in", "w1_in", "w2_in"))
            mask_in = [sem(f"mask_in{i}") for i in range(MB)]
            k_in, q_in = sem("k_in"), sem("q_in")
            kcopy_done, krest_done, qsplit_done = sem("kcopy_done"), sem("krest_done"), sem("qsplit_done")
            ks_in = [sem(f"ks_in{i}") for i in range(HG)]
            qs_in = [sem(f"qs_in{i}") for i in range(HG)]
            shift_in = sem("shift_in")
            out_done = sem("out_done")
            consts = sem("consts")
            pool_step = sem("pool_step")
            dve_step = sem("dve_step")
            zeroed = sem("zeroed")
            misc_full = sem("misc_full")
            act_took = sem("act_took")
            dve_took = sem("dve_took")
            scored = sem("scored")
            masked_done = sem("masked_done")
            exp_done = sem("exp_done")
            pv_done = sem("pv_done")
            pv_taken = sem("pv_taken")
            ve_ready = sem("ve_ready")
            rstd_ready = sem("rstd_ready")
            xn1_ready = sem("xn1_ready")
            kstat_done = sem("kstat_done")
            ksplit_done = sem("ksplit_done")
            qhalf_ready = sem("qhalf_ready")
            ub_ready = sem("ub_ready")
            shift_ready = sem("shift_ready")
            xn2_ready = sem("xn2_ready")
            sq_done = sem("sq_done")
            sq_pool = sem("sq_pool")
            rnorm_ready = sem("rnorm_ready")
            diff_ready = sem("diff_ready")
            ediff_ready = sem("ediff_ready")
            comb_ready = sem("comb_ready")
            ffn_full = sem("ffn_full")
            gelu_done = sem("gelu_done")
            down_taken = sem("down_taken")
            result_ready = sem("result_ready")
            sn_ready = sem("sn_ready")
            rsim_ready = sem("rsim_ready")
            fine_ready = sem("fine_ready")

            top_scored, top_masked = sem("top_scored"), sem("top_masked")
            top_turned, top_reduced = sem("top_turned"), sem("top_reduced")
            top_spread, top_back, top_taken = sem("top_spread"), sem("top_back"), sem("top_taken")

            block = ctx.enter_context(nc.Block())

            def rows(a, rep):
                return bass.AP(a.tensor, a.offset, [[0, rep]] + [list(d) for d in a.ap])

            @block.sync
            def _(sp):
                def load_ctx(b):
                    full = (NCH - 1) * P
                    if b > 0:
                        sp.wait_ge(misc_full, number["ctxT", b - 1, NK4 - 1] + 1)
                    sp.dma_start(ctx_nat[:, 0:NCH - 1, :],
                                 ctx_kv[b, 0:full, :].rearrange("(c p) d -> p c d", p=P)).then_inc(ctx_in, 16)
                    sp.dma_start(ctx_nat[0:KEYS[-1], NCH - 1, :], ctx_kv[b, full:KV, :]).then_inc(ctx_in, 16)

                def load_mask(b, i0, i1):
                    for i in range(i0, i1):
                        n = b * NM2 + i
                        if n >= MB:
                            sp.wait_ge(misc_full, number["maskT", (n - MB) // NM2, (n - MB) % NM2] + 1)
                        k0, k1 = 2 * i * P, min(2 * (i + 1) * P, KV)
                        sp.dma_start(mask_nat[:, n % MB, :, 0:k1 - k0],
                                     mask[b, 0].rearrange("(t p) k -> p t k", p=P)[:, :, k0:k1]).then_inc(mask_in[n % MB], 16)

                def stack_keys(b, hg):
                    sp.wait_ge(ksplit_done, b + 1)
                    if b > 0:
                        sp.wait_ge(scored, (b - 1) * SLOTS + (hg + 1) * NCH)
                    for pair in (2 * hg, 2 * hg + 1):
                        for t, (kp, _) in enumerate(TERMS):
                            sp.dma_start(kstack[t * PR:(t + 1) * PR, pair, :],
                                         kpart[kp][pair * PR:(pair + 1) * PR, :]).then_inc(ks_in[hg], 16)

                def place_shift(b):
                    sp.wait_ge(shift_ready, b + 1)
                    for i in range(PARTS):
                        sp.dma_start(qstack[CROW + i:CROW + i + 1, b].rearrange("o p a s -> o (p a) s"),
                                     shift_part[i][:, :]).then_inc(shift_in, 16)

                load_ctx(0)
                sp.dma_start(wk[:, :], Wk).then_inc(k_in, 16)
                sp.dma_start(bias_rows[0:EF, :], b1.rearrange("e (c p) -> (e c) p", p=P)).then_inc(k_in, 16)
                sp.dma_start(bias_rows[EF:EF + 1, :], rows(bq, 1)).then_inc(k_in, 16)
                sp.dma_start(bias_rows[EF + 1:EF + 2, :], rows(bk, 1)).then_inc(k_in, 16)
                load_mask(0, 0, MB)
                stack_keys(0, 0)
                place_shift(0)
                load_mask(0, MB, NM2)
                stack_keys(0, 1)
                stack_keys(0, 2)
                stack_keys(0, 3)
                for b in range(B):
                    if b == 0:
                        load_ctx(1)
                        sp.dma_start(w1[:, :, :], W1.rearrange("e d f -> d e f")).then_inc(w1_in, 16)
                        for hg in range(HG):
                            sp.wait_ge(qs_in[hg], 16 * 2 * len(TERMS))
                        sp.dma_start(w2[:, :, :], W2.rearrange("e (c p) d -> p (e c) d", p=P)).then_inc(w2_in, 16)
                    if b + 1 < B:
                        stack_keys(b + 1, 0)
                        stack_keys(b + 1, 1)
                        if b + 2 < B:
                            load_ctx(b + 2)
                        place_shift(b + 1)
                        load_mask(b + 1, 0, NM2)
                        stack_keys(b + 1, 2)
                        stack_keys(b + 1, 3)
                    if b > 0:
                        sp.wait_ge(result_ready, b)
                        sp.dma_start(out[b - 1].rearrange("(t p) d -> p t d", p=P),
                                     xs[:, (b - 1) * TT:b * TT, :]).then_inc(out_done, 16)
                sp.wait_ge(result_ready, B)
                sp.dma_start(out[B - 1].rearrange("(t p) d -> p t d", p=P), xs[:, (B - 1) * TT:, :]).then_inc(out_done, 16)
                sp.wait_ge(out_done, 16 * B)

            @block.gpsimd
            def _(pool):
                chain = [0]

                def link(ins):
                    chain[0] += 1
                    ins.then_inc(pool_step, 1)
                    pool.wait_ge(pool_step, chain[0])

                link(nc.gpsimd.memset(ident[:, :], 0.0))
                nc.gpsimd.affine_select(out=ident[:, :], in_=ident[:, :], compare_op=ALU.not_equal, fill=1.0, base=0,
                                        pattern=[[-1, P]], channel_multiplier=1).then_inc(consts, 1)
                link(nc.gpsimd.memset(minus_half[:, :], -0.5))
                nc.gpsimd.memset(kstack_flat[CROW:KROWS, :].bitcast(U32),
                                 0x3F803F80).then_inc(consts, 1)
                pool.wait_ge(consts, 2)
                link(nc.gpsimd.memset(blk[:, :], 1.0))
                link(nc.gpsimd.affine_select(out=blk[:, :], in_=blk[:, :], compare_op=ALU.is_ge, fill=0.0, base=0,
                                             pattern=[[-HD, H]], channel_multiplier=1))
                nc.gpsimd.affine_select(out=blk[:, :], in_=blk[:, :], compare_op=ALU.is_ge, fill=0.0, base=HD - 1,
                                        pattern=[[HD, H]], channel_multiplier=-1).then_inc(consts, 1)
                nc.gpsimd.iota(iota8[:, :], pattern=[[1, E]], base=0, channel_multiplier=0,
                               allow_small_or_imprecise_dtypes=True).then_inc(consts, 1)
                pool.wait_ge(ve_ready, 1)
                nc.gpsimd.tensor_tensor(rstd[:, :], var_eps[:, :], minus_half[:, :], ALU.pow).then_inc(rstd_ready, 1)

                def split_keys(b):
                    pool.wait_ge(act_took, by_scalar[number["kT", b, NK4 - 1]])
                    if b > 0:
                        pool.wait_ge(ks_in[HG - 1], 16 * 2 * len(TERMS) * b)
                    link(nc.gpsimd.tensor_copy(kpart[0][:, :], kT[:, :]))
                    pool.wait_ge(kstat_done, b + 1)
                    link(nc.gpsimd.tensor_tensor(kT[:, :], kT[:, :], kpart[0][:, :], ALU.subtract))
                    link(nc.gpsimd.tensor_copy(kpart[1][:, :], kT[:, :]))
                    nc.gpsimd.tensor_tensor(kpart[2][:, :], kT[:, :], kpart[1][:, :],
                                            ALU.subtract).then_inc(ksplit_done, 1)

                pool.wait_ge(qhalf_ready, 2 * PARTS)
                for hg in range(HG):
                    for pair in (2 * hg, 2 * hg + 1):
                        for t, (_, qp) in enumerate(TERMS):
                            pool.dma_start(qstack[t * PR:(t + 1) * PR, :, pair],
                                           qhalf[qp][pair * PR:(pair + 1) * PR]).then_inc(qs_in[hg], 16)
                pool.wait_ge(sq_pool, 1)
                nc.gpsimd.tensor_tensor(tiny[0:E, 3:4], tiny[0:E, 2:3], minus_half[0:E, 0:1],
                                        ALU.pow).then_inc(rsim_ready, 1)
                for b in range(B + 1):
                    if b > 0:
                        pool.wait_ge(ve_ready, b + 1)
                        nc.gpsimd.tensor_tensor(rstd[:, 0:TT], var_eps[:, 0:TT], minus_half[:, 0:TT],
                                                ALU.pow).then_inc(rstd_ready, 1)
                    if b > 0:
                        pool.wait_ge(sq_pool, b + 1)
                        nc.gpsimd.tensor_tensor(rnorm[:, :], sumsq[:, :], minus_half[:, 0:TT],
                                                ALU.pow).then_inc(rnorm_ready, 1)
                    if b + 1 < B:
                        split_keys(b + 1)

            @block.tensor
            def _(pe):
                ffn_uses = [0]
                ffn_owner = []

                def ffn_bank():
                    n = ffn_uses[0]
                    ffn_uses[0] += 1
                    if n >= 2:
                        who, count = ffn_owner[n - 2]
                        pe.wait_ge(gelu_done if who == "gelu" else down_taken, count)
                    return ffn[n % 2]

                def misc_step(n, kind, b, i):
                    m = used_before(n)
                    if m is not None:
                        if steps[m][0] in BY_SCALAR:
                            pe.wait_ge(act_took, by_scalar[m])
                        else:
                            pe.wait_ge(dve_took, by_vector[m])
                    misc = bank_of(n)
                    last = None
                    if kind == "bias":
                        pe.wait_ge(k_in, 16 * 4)
                        pe.wait_ge(consts, 2)
                        last = nc.tensor.transpose(misc[:, 0:EF + 2], bias_rows[:, :], ident[0:EF + 2, 0:EF + 2])
                    elif kind == "xnT0":
                        pe.wait_ge(xn1_ready, 4 * (i + 1))
                        for j in range(4):
                            c = 4 * i + j
                            last = nc.tensor.transpose(misc[:, j * P:(j + 1) * P], xn1[:, c * D:(c + 1) * D], ident[:, :])
                    elif kind == "q":
                        pe.wait_ge(q_in, 16)
                        pe.wait_ge(dve_took, by_vector[number["xnT0", 0, i]])
                        last = nc.tensor.matmul(misc[:, :], wq[:, :], xn1T[:, i * BANK:(i + 1) * BANK],
                                                start=True, stop=True)
                    elif kind == "ctxT":
                        pe.wait_ge(ctx_in, 32 * (b + 1))
                        for j, c in enumerate(range(4 * i, min(4 * i + 4, NCH))):
                            k = KEYS[c]
                            last = nc.tensor.transpose(misc[:, j * P:j * P + k], ctx_nat[0:k, c, :], ident[0:k, 0:k])
                    elif kind == "kT":
                        pe.wait_ge(act_took, by_scalar[number["ctxT", b, NK4 - 1]])
                        k0, k1 = i * BANK, min((i + 1) * BANK, KV)
                        last = nc.tensor.matmul(misc[:, 0:k1 - k0], wk[:, :], ctxT[:, k0:k1], start=True, stop=True)
                    elif kind == "v":
                        if b == 0:
                            pe.wait_ge(w_in, 16 * 8)
                        pe.wait_ge(act_took, by_scalar[number["ctxT", b, NK4 - 1]])
                        for j, c in enumerate(range(4 * i, min(4 * i + 4, NCH))):
                            k = KEYS[c]
                            last = nc.tensor.matmul(misc[0:k, j * P:(j + 1) * P], ctxT[:, c * P:c * P + k], wv[:, :],
                                                    start=True, stop=True)
                    elif kind == "maskT":
                        n4 = b * NM2 + i
                        pe.wait_ge(mask_in[n4 % MB], 16 * (n4 // MB + 1))
                        for j, c in enumerate(range(2 * i, min(2 * i + 2, NCH))):
                            k = KEYS[c]
                            for t in range(TT):
                                at = j * S + t * P
                                last = nc.tensor.transpose(misc[0:k, at:at + P], mask_nat[:, n4 % MB, t, j * P:j * P + k],
                                                           ident[:, :])
                    elif kind == "shift":
                        pe.wait_ge(ub_ready, b + 1)
                        last = nc.tensor.matmul(misc[0:H, 0:S], negblk[:, :], ub[:, :], start=True, stop=True)
                    elif kind == "simT":
                        pe.wait_ge(sn_ready, 1)
                        last = nc.tensor.transpose(misc[:, 0:E], sim_rows[:, :], ident[0:E, 0:E])
                    elif kind == "WpT":
                        last = nc.tensor.transpose(misc[:, 0:D], wp[:, :], ident[:, :])
                    elif kind == "WpSim":
                        pe.wait_ge(dve_took, by_vector[number["simT", 0, 0]])
                        last = nc.tensor.matmul(misc[:, 0:E], wp[:, :], simT[:, :], start=True, stop=True)
                    elif kind == "oT":
                        pe.wait_ge(pv_taken, b * HG + i + 1)
                        for t in range(TT):
                            last = nc.tensor.transpose(misc[:, t * P:(t + 1) * P], osum[:, t * P:(t + 1) * P], ident[:, :])
                    elif kind == "verdict":
                        pe.wait_ge(fine_ready, 1)
                        last = nc.tensor.transpose(misc[0:1, 0:P], fine[:, 0:1], ident[:, :])
                    elif kind == "onT":
                        pe.wait_ge(dve_took, by_vector[number["oT", b, HG - 1]])
                        for t in range(TT):
                            last = nc.tensor.transpose(misc[:, t * P:(t + 1) * P],
                                                       onat[:, t].rearrange("p h d -> p (h d)"), ident[:, :])
                    elif kind == "wo":
                        pe.wait_ge(act_took, by_scalar[number["onT", b, 0]])
                        for t in range(TT):
                            last = nc.tensor.matmul(misc[:, t * D:(t + 1) * D], onT[:, t * P:(t + 1) * P], wo[:, :],
                                                    start=True, stop=True)
                    elif kind == "xnT":
                        pe.wait_ge(xn2_ready, b + 1)
                        for t in range(TT):
                            last = nc.tensor.transpose(misc[:, t * P:(t + 1) * P], xn2[:, t, :], ident[:, :])
                    elif kind == "gate":
                        pe.wait_ge(dve_took, by_vector[number["xnT", b, 0]])
                        for t in range(TT):
                            last = nc.tensor.matmul(misc[:, t * GW:(t + 1) * GW], xn2T[:, t * P:(t + 1) * P], wg[:, :],
                                                    start=True, stop=True)
                    elif kind == "combT":
                        pe.wait_ge(comb_ready, b + 1)
                        for t in range(TT):
                            last = nc.tensor.transpose(misc[0:E, t * P:(t + 1) * P], comb[:, t, :], ident[:, :])
                    elif kind == "b2":
                        pe.wait_ge(dve_took, by_vector[number["combT", b, 0]])
                        for t in range(TT):
                            last = nc.tensor.matmul(misc[:, t * D:(t + 1) * D], combT[:, t * P:(t + 1) * P],
                                                    b2_rows[:, :], start=True, stop=True)
                    last.then_inc(misc_full, 1)

                def stacked(b, hg):
                    pe.wait_ge(ks_in[hg], 16 * 2 * len(TERMS) * (b + 1))
                    if b == 0:
                        pe.wait_ge(qs_in[hg], 16 * 2 * len(TERMS))
                    if hg == 0:
                        pe.wait_ge(shift_in, 16 * PARTS * (b + 1))

                def products(b, hg, ch, to):
                    k = KEYS[ch]
                    for j in range(2):
                        pair = 2 * hg + j
                        last = nc.tensor.matmul(to[0:k, j * BANK:(j + 1) * BANK],
                                                kstack[:, pair, ch * P:ch * P + k],
                                                qstack[:, b, pair].rearrange("r a s -> r (a s)"),
                                                start=True, stop=True)
                    return last

                def scores(b, hg, ch):
                    g = b * SLOTS + hg * NCH + ch
                    if ch == 0:
                        stacked(b, hg)
                    if g >= 2:
                        pe.wait_ge(masked_done, g - 1)
                    if exact and ch == 0:
                        pe.wait_ge(top_taken, b * HG + hg + 1)
                    products(b, hg, ch, score[g % 2]).then_inc(scored, 1)

                def largest(b, hg):
                    hgn = b * HG + hg
                    stacked(b, hg)
                    if hgn > 0:
                        pe.wait_ge(masked_done, hgn * NCH)
                    for ch in range(NCH):
                        n = hgn * NCH + ch
                        products(b, hg, ch, score[0]).then_inc(top_scored, 1)
                        pe.wait_ge(top_masked, n + 1)
                        k = KEYS[ch]
                        for j in range(2 * 4):
                            last = nc.tensor.transpose(score[1][:, j * P:j * P + k],
                                                       masked[0:k, 0, j * P:(j + 1) * P], ident[0:k, 0:k])
                        last.then_inc(top_turned, 1)
                        pe.wait_ge(top_reduced, n + 1)
                    pe.wait_ge(top_spread, hgn + 1)
                    for j in range(2 * 4):
                        last = nc.tensor.transpose(score[1][:, j * P:(j + 1) * P], masked[:, 0, j * P:(j + 1) * P],
                                                   ident[:, :])
                    last.then_inc(top_back, 1)

                def values(g):
                    b, hg, ch = g // SLOTS, g % SLOTS // NCH, g % NCH
                    if ch == 0 and g > 0:
                        pe.wait_ge(pv_taken, g // NCH)
                    pe.wait_ge(exp_done, g + 1)
                    k = KEYS[ch]
                    for j in range(4):
                        last = nc.tensor.matmul(pv[32 * j:32 * j + HD + 1, 0:S], vals[0:k, ch, 4 * hg + j, :],
                                                probs[0:k, g % 2, j * S:(j + 1) * S], start=(ch == 0),
                                                stop=(ch == NCH - 1), tile_position=(0, 32 * j))
                    last.then_inc(pv_done, 1)

                def up(b, h):
                    if b == 0 and h == 0:
                        pe.wait_ge(w1_in, 16)
                    for i in range(0, HALF * FC, 2):
                        bank = ffn_bank()
                        for j in range(2):
                            e, c = h * HALF + (i + j) // FC, (i + j) % FC
                            last = nc.tensor.matmul(bank[:, j * S:(j + 1) * S], w1[:, e, c * P:(c + 1) * P], xn2T[:, :],
                                                    start=True, stop=True)
                        last.then_inc(ffn_full, 1)
                        ffn_owner.append(("gelu", (2 * b + h) * UPS + i // 2 + 1))

                def down(b, h, u):
                    e, t = u // TT, u % TT
                    if u == 0:
                        pe.wait_ge(gelu_done, (2 * b + h + 1) * UPS)
                        if b == 0 and h == 0:
                            pe.wait_ge(w2_in, 16)
                    bank = ffn_bank()
                    for c in range(FC):
                        last = nc.tensor.matmul(bank[:, 0:D], hid[:, e * FC + c, t * P:(t + 1) * P],
                                                w2[:, (h * HALF + e) * FC + c, :], start=(c == 0), stop=(c == FC - 1))
                    last.then_inc(ffn_full, 1)
                    ffn_owner.append(("down", (2 * b + h) * DOWNS + u + 1))

                for n, (kind, b, i) in enumerate(before):
                    misc_step(n, kind, b, i)
                    pe.wait_ge(zeroed, 1)
                pe.wait_ge(act_took, by_scalar[len(before) - 1])
                pe.wait_ge(dve_took, by_vector[len(before) - 1])
                for b in range(B):
                    for slot in range(SLOTS):
                        g = b * SLOTS + slot
                        for step in at_slot[b, slot]:
                            misc_step(*step)
                        if exact and slot % NCH == 0:
                            largest(b, slot // NCH)
                        scores(b, slot // NCH, slot % NCH)
                        if g >= LAG:
                            values(g - LAG)
                        for h in range(2):
                            if b > 0 and slot == BURST[h]:
                                up(b - 1, h)
                            if b > 0 and slot in range(DOWN[h], DOWN[h] + 2 * DOWNS, 2):
                                down(b - 1, h, (slot - DOWN[h]) // 2)
                for g in range(B * SLOTS - LAG, B * SLOTS):
                    values(g)
                for n in range(first_after, len(steps)):
                    misc_step(n, *steps[n])
                    if steps[n][0] == "gate":
                        up(B - 1, 0)
                for u in range(DOWNS):
                    down(B - 1, 0, u)
                up(B - 1, 1)
                for u in range(DOWNS):
                    down(B - 1, 1, u)

            @block.scalar
            def _(act):
                def misc_step(n, kind, b, i):
                    misc = bank_of(n)
                    if kind in BY_SCALAR:
                        act.wait_ge(misc_full, n + 1)
                    if kind == "ctxT":
                        if b > 0 and i == 0:
                            act.wait_ge(misc_full, number["v", b - 1, NK4 - 1] + 1)
                        k0, k1 = i * BANK, min((i + 1) * BANK, KV)
                        nc.scalar.activation(ctxT[:, k0:k1], misc[:, 0:k1 - k0], ACT.Copy).then_inc(act_took, 1)
                    elif kind == "kT":
                        if b > 0 and i == 0:
                            act.wait_ge(ksplit_done, b)
                        elif b == 0 and i == 0:
                            act.wait_ge(dve_took, 1)
                        k0, k1 = i * BANK, min((i + 1) * BANK, KV)
                        nc.scalar.activation(kT[:, k0:k1], misc[:, 0:k1 - k0], ACT.Identity,
                                             bias=bias_cols[:, EF + 1:EF + 2]).then_inc(act_took, 1)
                    elif kind == "maskT":
                        c0, c1 = 2 * i, min(2 * i + 2, NCH)
                        if b > 0:
                            act.wait_ge(masked_done, b * SLOTS - NCH + c1)
                        k = KEYS[c1 - 1]
                        nc.scalar.activation(maskT[0:k, c0:c1, :].rearrange("p c s -> p (c s)"),
                                             misc[0:k, 0:(c1 - c0) * S], ACT.Copy, scale=MASK_SCALE).then_inc(act_took, 1)
                    elif kind == "onT":
                        nc.scalar.activation(onT[:, :], misc[:, 0:S], ACT.Copy).then_inc(act_took, 1)
                    elif kind == "gate":
                        act.wait_ge(misc_full, n + 1)
                        for t in range(TT):
                            nc.scalar.activation(junk[:, :], misc[:, t * GW:t * GW + D], ACT.Square,
                                                 accum_out=sumsq[:, t:t + 1]).then_inc(sq_done, 1)
                            act.wait_ge(sq_done, b * TT + t + 1)

                def weigh(b):
                    act.wait_ge(diff_ready, b + 1)
                    nc.scalar.activation(ediff[:, :], diff[:, :], ACT.Exp).then_inc(ediff_ready, 1)

                def exps(g):
                    k = KEYS[g % NCH]
                    act.wait_ge(masked_done, g + 1)
                    if g >= 2:
                        act.wait_ge(pv_done, g - 1)
                    nc.scalar.activation(probs[0:k, g % 2, :], masked[0:k, g % 2, :], ACT.Exp).then_inc(exp_done, 1)

                def gelus(b, h):
                    if b > 0 or h > 0:
                        act.wait_ge(ffn_full, (2 * b + h) * (UPS + DOWNS))
                    for n in range(UPS):
                        use = (2 * b + h) * (UPS + DOWNS) + n
                        act.wait_ge(ffn_full, use + 1)
                        for j in range(2):
                            i = 2 * n + j
                            k = h * HALF * FC + i
                            last = nc.scalar.activation(hid[:, i, :], ffn[use % 2][:, j * S:(j + 1) * S], ACT.Gelu,
                                                        bias=bias_cols[:, k:k + 1])
                        last.then_inc(gelu_done, 1)

                act.dma_start(xs[:, :, :], x.rearrange("b (t p) d -> p (b t) d", p=P)).then_inc(x_in, 16)
                act.dma_start(wq[:, :], Wq).then_inc(q_in, 16)
                for dst, src in ((wv[:, :], Wv), (bv_all[:, :], rows(bv, P)), (bo_all[:, :], rows(bo, P)),
                                 (b2_rows[:, :], b2), (sim_rows[:, :], sim), (wp[:, :], Wp), (wo[:, :], Wo),
                                 (tiny[:, 0:1], bass.AP(temp.tensor, temp.offset, [[0, P], [1, 1]]))):
                    act.dma_start(dst, src).then_inc(w_in, 16)
                for n, (kind, b, i) in enumerate(before):
                    misc_step(n, kind, b, i)
                    if kind == "kT" and i == NK4 - 1:
                        act.wait_ge(act_took, by_scalar[n])
                        nc.scalar.activation(kpart[0][:, :], kT[:, :], ACT.Copy).then_inc(kcopy_done, 1)
                    if kind == "q" and i == B * S // BANK - 1:
                        act.wait_ge(qsplit_done, 1)
                        for part in range(PARTS):
                            for a in range(2):
                                nc.scalar.activation(qhalf[part][:, :, a, :],
                                                     qpart[part].rearrange("p (b s) -> p b s", b=B), ACT.Copy,
                                                     scale=half[:, a:a + 1]).then_inc(qhalf_ready, 1)
                    if kind == "shift":
                        act.wait_ge(krest_done, 1)
                        nc.scalar.activation(kpart[1][:, :], kT[:, :], ACT.Copy).then_inc(kcopy_done, 1)
                for b in range(B):
                    for slot in range(SLOTS):
                        for step in at_slot[b, slot]:
                            misc_step(*step)
                        if b * SLOTS + slot > 0:
                            exps(b * SLOTS + slot - 1)
                        if b > 0 and slot == 15:
                            weigh(b - 1)
                        if b > 0 and slot in BURST:
                            gelus(b - 1, BURST.index(slot))
                exps(B * SLOTS - 1)
                for n in range(first_after, len(steps)):
                    misc_step(n, *steps[n])
                weigh(B - 1)
                gelus(B - 1, 0)
                gelus(B - 1, 1)

            @block.vector
            def _(dve):
                chain = [0]

                def link(ins):
                    chain[0] += 1
                    ins.then_inc(dve_step, 1)
                    dve.wait_ge(dve_step, chain[0])

                def moments_of(tile, n):
                    link(nc.vector.bn_stats(stats[:, n, :], tile))
                    link(nc.vector.bn_aggr(moments[:, n, :], stats[:, n, :]))

                def split_keys_first():
                    dve.wait_ge(kcopy_done, 1)
                    dve.wait_ge(kstat_done, 1)
                    nc.vector.tensor_tensor(kT[:, :], kT[:, :], kpart[0][:, :], ALU.subtract).then_inc(krest_done, 1)
                    bound(0)
                    dve.wait_ge(kcopy_done, 2)
                    nc.vector.tensor_tensor(kpart[2][:, :], kT[:, :], kpart[1][:, :],
                                            ALU.subtract).then_inc(ksplit_done, 1)

                def key_extremes(b):
                    dve.wait_ge(act_took, by_scalar[number["kT", b, NK4 - 1]])
                    nc.vector.tensor_reduce(kmax[:, :], kT[:, :], AX_X, ALU.max,
                                            apply_absolute_value=True).then_inc(kstat_done, 1)

                def bound(b):
                    dve.wait_ge(kstat_done, b + 1)
                    link(nc.vector.tensor_scalar(ub[:, :], qs[:, b * S:(b + 1) * S], kmax[:, :], None, ALU.mult))
                    nc.vector.scalar_tensor_tensor(out=ub[:, :], in0=ub[:, :], scalar=-1.0, in1=ub[:, :],
                                                   op0=ALU.mult, op1=ALU.max).then_inc(ub_ready, 1)

                def misc_step(n, kind, b, i):
                    if kind in BY_SCALAR:
                        return
                    misc = bank_of(n)
                    dve.wait_ge(misc_full, n + 1)
                    if kind == "verdict":
                        nc.vector.tensor_reduce(fine[0:1, 1:2], misc[0:1, 0:P], AX_X, ALU.min).then_inc(dve_took, 1)
                        dve.wait_ge(dve_took, by_vector[n])
                        link(nc.vector.tensor_scalar(verdict[:, 0:1], fine[0:1, 1:2], 0.5, None, ALU.is_lt))
                    elif kind == "bias":
                        nc.vector.tensor_copy(bias_cols[:, :], misc[:, 0:EF + 2]).then_inc(dve_took, 1)
                    elif kind == "xnT0":
                        nc.vector.tensor_copy(xn1T[:, i * BANK:(i + 1) * BANK], misc[:, :]).then_inc(dve_took, 1)
                    elif kind == "q":
                        if i == 0:
                            dve.wait_ge(dve_took, 1)
                        sl = slice(i * BANK, (i + 1) * BANK)
                        nc.vector.tensor_scalar(qs[:, sl], misc[:, :], bias_cols[:, EF:EF + 1], INV_SQRT_D, ALU.add,
                                                ALU.mult).then_inc(dve_took, 1)
                        if i == B * S // BANK - 1:
                            dve.wait_ge(dve_took, by_vector[n])
                            link(nc.vector.tensor_copy(qpart[0], qs[:, :]))
                            link(nc.vector.tensor_tensor(qrest, qs[:, :], qpart[0], ALU.subtract))
                            link(nc.vector.tensor_copy(qpart[1], qrest))
                            nc.vector.tensor_tensor(qpart[2], qrest, qpart[1], ALU.subtract).then_inc(qsplit_done, 1)
                    elif kind == "v":
                        c0, c1 = 4 * i, min(4 * i + 4, NCH)
                        k = KEYS[c1 - 1]
                        w = c1 - c0
                        bvv = bv_all[0:k, :].rearrange("p (h d) -> p h d", d=HD)
                        bvv = bass.AP(bvv.tensor, bvv.offset, [list(bvv.ap[0]), [0, w]] + [list(d) for d in bvv.ap[1:]])
                        nc.vector.tensor_tensor(vals[0:k, c0:c1, :, 0:HD],
                                                misc[0:k, 0:w * D].rearrange("p (c h d) -> p c h d", c=w, d=HD),
                                                bvv, ALU.add).then_inc(dve_took, 1)
                    elif kind == "shift":
                        if b > 0:
                            dve.wait_ge(shift_in, 16 * PARTS * b)
                        if exact:
                            nc.vector.memset(shift[:, :], 0.0).then_inc(dve_took, 1)
                        else:
                            nc.vector.tensor_copy(shift[:, :], misc[0:H, 0:S]).then_inc(dve_took, 1)
                        dve.wait_ge(dve_took, by_vector[n])
                        link(nc.vector.tensor_copy(shift_part[0][:, :], shift[:, :]))
                        link(nc.vector.tensor_tensor(shift[:, :], shift[:, :], shift_part[0][:, :], ALU.subtract))
                        link(nc.vector.tensor_copy(shift_part[1][:, :], shift[:, :]))
                        nc.vector.tensor_tensor(shift_part[2][:, :], shift[:, :], shift_part[1][:, :],
                                                ALU.subtract).then_inc(shift_ready, 1)
                    elif kind == "simT":
                        nc.vector.tensor_copy(simT[:, :], misc[:, 0:E]).then_inc(dve_took, 1)
                    elif kind == "WpT":
                        nc.vector.tensor_copy(wg[:, 0:D], misc[:, 0:D]).then_inc(dve_took, 1)
                    elif kind == "WpSim":
                        nc.vector.tensor_copy(wg[:, D:GW], misc[:, 0:E]).then_inc(dve_took, 1)
                    elif kind == "oT":
                        o = misc[:, 0:S].rearrange("p (t r) -> p t r", r=32)
                        inv = inverses[:, b * HG + i]
                        flat_inv = inv.rearrange("p t j -> p (t j)")
                        link(nc.vector.tensor_scalar(flat_inv, o[:, :, HD], SUM_FLOOR, None, ALU.max))
                        link(nc.vector.reciprocal(flat_inv, flat_inv))
                        if i == 0 and b > 0:
                            dve.wait_ge(misc_full, number["onT", b - 1, 0] + 1)
                        r = bass.AP(inv.tensor, inv.offset, [list(d) for d in inv.ap] + [[0, HD]])
                        nc.vector.tensor_tensor(onat[:, :, 4 * i:4 * i + 4, :],
                                                misc[:, 0:S].rearrange("p (t j r) -> p t j r", t=TT, r=32)[:, :, :, 0:HD],
                                                r, ALU.mult).then_inc(dve_took, 1)
                    elif kind == "wo":
                        at = slice(b * TT, (b + 1) * TT)
                        nc.vector.tensor_tensor(xs[:, at, :], xs[:, at, :],
                                                misc[:, 0:TT * D].rearrange("p (t d) -> p t d", t=TT),
                                                ALU.add).then_inc(dve_took, 1)
                        dve.wait_ge(dve_took, by_vector[n])
                        for t in range(TT):
                            moments_of(xs[:, b * TT + t, :], t)
                        nc.vector.tensor_scalar(var_eps[:, 0:TT], moments[:, 0:TT, 1], LN_EPS, None,
                                                ALU.add).then_inc(ve_ready, 1)
                    elif kind == "xnT":
                        nc.vector.tensor_copy(xn2T[:, :], misc[:, 0:S]).then_inc(dve_took, 1)
                    elif kind == "gate":
                        dve.wait_ge(sq_done, TT * (b + 1))
                        nc.vector.tensor_copy(graw[:, :, :], misc[:, 0:TT * GW].rearrange(
                            "p (t g) -> p t g", t=TT)[:, :, D:GW]).then_inc(dve_took, 1)
                        nc.vector.tensor_scalar(sumsq[:, :], sumsq[:, :], L2_EPS ** 2, None, ALU.max).then_inc(sq_pool, 1)
                    elif kind == "combT":
                        nc.vector.tensor_copy(combT[:, :], misc[0:E, 0:S]).then_inc(dve_took, 1)
                    elif kind == "b2":
                        at = slice(b * TT, (b + 1) * TT)
                        nc.vector.tensor_tensor(xs[:, at, :], xs[:, at, :],
                                                misc[:, 0:TT * D].rearrange("p (t d) -> p t d", t=TT),
                                                ALU.add).then_inc(dve_took, 1)

                def normalise(b):
                    dve.wait_ge(rstd_ready, b + 2)
                    for t in range(TT):
                        last = nc.vector.tensor_scalar(xn2[:, t, :], xs[:, b * TT + t, :], moments[:, t, 0:1],
                                                       rstd[:, t:t + 1], ALU.subtract, ALU.mult)
                        if t < TT - 1:
                            link(last)
                    last.then_inc(xn2_ready, 1)

                def choose(b):
                    dve.wait_ge(rnorm_ready, b + 1)
                    for t in range(TT):
                        link(nc.vector.tensor_scalar(gsc[:, t, :], graw[:, t, :], rnorm[:, t:t + 1], tiny[:, 1:2],
                                                     ALU.mult, ALU.mult))
                        link(nc.vector.max(top[:, t, :], gsc[:, t, :]))
                        link(nc.vector.max_index(topi[:, t, :], top[:, t, :], gsc[:, t, :]))
                    link(nc.vector.tensor_copy(topf[:, :, :], topi[:, :, :]))
                    nc.vector.tensor_tensor(diff[:, :], top[:, :, 1], top[:, :, 0], ALU.subtract).then_inc(diff_ready, 1)

                def combine(b):
                    dve.wait_ge(ediff_ready, b + 1)
                    link(nc.vector.tensor_scalar(den[:, :], ediff[:, :], 1.0, None, ALU.add))
                    link(nc.vector.reciprocal(p1[:, :], den[:, :]))
                    link(nc.vector.tensor_tensor(p2[:, :], ediff[:, :], p1[:, :], ALU.mult))
                    for t in range(TT):
                        link(nc.vector.tensor_scalar(hot[:, :], iota8[:, :], topf[:, t, 0:1], p1[:, t:t + 1],
                                                     ALU.is_equal, ALU.mult))
                        link(nc.vector.tensor_scalar(comb[:, t, :], iota8[:, :], topf[:, t, 1:2], p2[:, t:t + 1],
                                                     ALU.is_equal, ALU.mult))
                        link(nc.vector.tensor_tensor(comb[:, t, :], comb[:, t, :], hot[:, :], ALU.add))
                    dve.sem_inc(comb_ready, 1)

                def norm_sim():
                    link(nc.vector.reciprocal(tiny[:, 1:2], tiny[:, 0:1]))
                    link(nc.vector.tensor_tensor(junk[0:E, :], sim_rows[:, :], sim_rows[:, :], ALU.mult))
                    link(nc.vector.tensor_reduce(tiny[0:E, 4:5], junk[0:E, :], AX_X, ALU.add))
                    nc.vector.tensor_scalar(tiny[0:E, 2:3], tiny[0:E, 4:5], L2_EPS ** 2, None,
                                            ALU.max).then_inc(sq_pool, 1)
                    bov = bass.AP(bo_all[:, :].tensor, bo_all[:, :].offset,
                                  [list(bo_all[:, :].ap[0]), [0, NT], [1, D]])
                    dve.wait_ge(xn1_ready, NT)
                    link(nc.vector.tensor_tensor(xs[:, :, :], xs[:, :, :], bov, ALU.add))

                def scale_sim():
                    dve.wait_ge(rsim_ready, 1)
                    nc.vector.tensor_scalar(sim_rows[:, :], sim_rows[:, :], tiny[0:E, 3:4], None,
                                            ALU.mult).then_inc(sn_ready, 1)

                def masked_scores(scores, half_, ch):
                    k = KEYS[ch]
                    m = maskT[0:k, ch, :]
                    m4 = bass.AP(m.tensor, m.offset, [list(m.ap[0]), [0, 4], list(m.ap[1])])
                    return nc.vector.tensor_tensor(masked[0:k, half_, :].rearrange("p (h s) -> p h s", h=4),
                                                   scores[0:k, :].rearrange("p (h s) -> p h s", h=4), m4, ALU.add)

                def judge():
                    flat_inv = inverses[:, :, :, :].rearrange("p g t j -> p (g t j)")
                    link(nc.vector.tensor_scalar(top_rows[:, 0:B * HG * TT * 4], flat_inv, 1.0 / SUM_LEAST, None, ALU.is_lt))
                    link(nc.vector.tensor_scalar(flat_inv, flat_inv, 1.0 / SUM_MOST, None, ALU.is_gt))
                    link(nc.vector.tensor_tensor(flat_inv, flat_inv, top_rows[:, 0:B * HG * TT * 4], ALU.min))
                    nc.vector.tensor_reduce(fine[:, 0:1], flat_inv, AX_X, ALU.min).then_inc(fine_ready, 1)

                def add_mask(g):
                    b, ch = g // SLOTS, g % NCH
                    k = KEYS[ch]
                    dve.wait_ge(scored, g + 1)
                    if g % SLOTS < NCH:
                        dve.wait_ge(act_took, by_scalar[number["maskT", b, ch // 2]])
                    if g >= 2:
                        dve.wait_ge(exp_done, g - 1)
                    last = masked_scores(score[g % 2], g % 2, ch)
                    if exact:
                        link(last)
                        last = nc.vector.tensor_tensor(masked[0:k, g % 2, :], masked[0:k, g % 2, :], top_rows[0:k, :],
                                                       ALU.subtract)
                    last.then_inc(masked_done, 1)

                def largest(b, hg):
                    hgn = b * HG + hg
                    if hg == 0:
                        dve.wait_ge(act_took, by_scalar[number["maskT", b, NM2 - 1]])
                    if hgn > 0:
                        dve.wait_ge(exp_done, hgn * NCH)
                    for ch in range(NCH):
                        n = hgn * NCH + ch
                        k = KEYS[ch]
                        dve.wait_ge(top_scored, n + 1)
                        masked_scores(score[0], 0, ch).then_inc(top_masked, 1)
                        dve.wait_ge(top_turned, n + 1)
                        turned = score[1][:, :].rearrange("p (j k) -> p j k", k=P)[:, :, 0:k]
                        link(nc.vector.tensor_reduce(top_score[:, min(ch, 1), :], turned, AX_X, ALU.max))
                        if ch > 0:
                            link(nc.vector.tensor_tensor(top_score[:, 0, :], top_score[:, 0, :], top_score[:, 1, :],
                                                         ALU.max))
                        dve.sem_inc(top_reduced, 1)
                    tops = top_score[:, 0, :]
                    nc.vector.tensor_copy(masked[:, 0, :].rearrange("p (j k) -> p j k", k=P),
                                          bass.AP(tops.tensor, tops.offset, [list(d) for d in tops.ap] + [[0, P]])
                                          ).then_inc(top_spread, 1)
                    dve.wait_ge(top_back, hgn + 1)
                    link(nc.vector.tensor_copy(top_rows[:, :], score[1][:, :]))
                    dve.sem_inc(top_taken, 1)

                def take_values(hgn):
                    dve.wait_ge(pv_done, (hgn + 1) * NCH)
                    if hgn > 0:
                        dve.wait_ge(misc_full, number["oT", (hgn - 1) // HG, (hgn - 1) % HG] + 1)
                    nc.vector.tensor_copy(osum[:, :], pv[:, 0:S]).then_inc(pv_taken, 1)

                def take_down(b, h, u):
                    e, t = h * HALF + u // TT, u % TT
                    use = (2 * b + h) * (UPS + DOWNS) + UPS + u
                    dve.wait_ge(ffn_full, use + 1)
                    taken = (2 * b + h) * DOWNS + u
                    if h == 0 and u == 0:
                        dve.wait_ge(dve_took, by_vector[number["b2", b, 0]])
                    if taken > 0:
                        dve.wait_ge(down_taken, taken)
                    n2 = b * TT + t
                    nc.vector.scalar_tensor_tensor(out=xs[:, n2, :], in0=ffn[use % 2][:, 0:D], scalar=comb[:, t, e:e + 1],
                                                   in1=xs[:, n2, :], op0=ALU.mult, op1=ALU.add).then_inc(down_taken, 1)

                link(nc.vector.memset(vals[:, :, :, HD:HD + 1], 1.0))
                nc.vector.memset(pv[:, :], 0.0).then_inc(zeroed, 1)
                dve.wait_ge(x_in, 16)
                for n in range(NT):
                    nc.vector.bn_stats(stats[:, n, :], xs[:, n, :]).then_inc(dve_step, 1)
                chain[0] += NT
                for n in range(NT):
                    dve.wait_ge(dve_step, chain[0] - NT + n + 1)
                    nc.vector.bn_aggr(moments[:, n, :], stats[:, n, :]).then_inc(dve_step, 1)
                chain[0] += NT
                dve.wait_ge(dve_step, chain[0])
                nc.vector.tensor_scalar(var_eps[:, :], moments[:, :, 1], LN_EPS, None, ALU.add).then_inc(ve_ready, 1)
                misc_step(0, *steps[0])
                dve.wait_ge(consts, 3)
                link(nc.vector.tensor_scalar(negblk[:, :], blk[:, :], -1.0, None, ALU.mult))
                for a in range(2):
                    link(nc.vector.tensor_reduce(half[:, a:a + 1], blk[:, :].rearrange("p (h a) -> p a h", a=2)[:, a, :],
                                                 AX_X, ALU.add))
                dve.wait_ge(rstd_ready, 1)
                for n in range(NT):
                    nc.vector.tensor_scalar(xn1[:, n * D:(n + 1) * D], xs[:, n, :], moments[:, n, 0:1],
                                            rstd[:, n:n + 1], ALU.subtract, ALU.mult).then_inc(xn1_ready, 1)
                for n, (kind, b, i) in enumerate(before):
                    if kind == "shift":
                        key_extremes(0)
                        split_keys_first()
                    if kind == "v" and i == 0:
                        dve.wait_ge(w_in, 16 * 8)
                    if n > 0:
                        misc_step(n, kind, b, i)
                dve.wait_ge(consts, 4)
                for b in range(B):
                    for slot in range(SLOTS):
                        g = b * SLOTS + slot
                        if slot % NCH == LAG and g > LAG:
                            take_values(g // NCH - 1)
                        for step in at_slot[b, slot]:
                            misc_step(*step)
                        if exact and slot % NCH == 0:
                            largest(b, slot // NCH)
                        add_mask(g)
                        if b == 0 and slot == 12:
                            norm_sim()
                        if b == 0 and slot == 25:
                            scale_sim()
                        if b + 1 < B and slot == 20:
                            key_extremes(b + 1)
                            bound(b + 1)
                        if b > 0:
                            if slot == 10:
                                normalise(b - 1)
                            if slot == 14:
                                choose(b - 1)
                            if slot == 16:
                                combine(b - 1)
                            for h in range(2):
                                if slot in range(DOWN[h], DOWN[h] + 2 * DOWNS, 2):
                                    take_down(b - 1, h, (slot - DOWN[h]) // 2)
                    if b > 0:
                        dve.wait_ge(down_taken, b * E * TT)
                        dve.sem_inc(result_ready, 1)
                take_values(B * HG - 1)
                for n in range(first_after, len(steps)):
                    if steps[n][0] == "verdict":
                        judge()
                    if steps[n][0] == "xnT":
                        normalise(B - 1)
                    if steps[n][0] == "combT":
                        choose(B - 1)
                        combine(B - 1)
                    misc_step(n, *steps[n])
                for h in range(2):
                    for u in range(DOWNS):
                        take_down(B - 1, h, u)
                dve.wait_ge(down_taken, B * E * TT)
                dve.sem_inc(result_ready, 1)

        with ExitStack() as own:
            attempt(own, False)
        redo = nc.values_load(verdict[0:1, 0:1], min_val=0, max_val=1)
        with nc.If(redo != 0):
            with ExitStack() as own:
                attempt(own, True)


_INS = ["x", "ctx_1024", "mask_Bx1xSxS2_ff0", "L0_xattn_Wq", "L0_xattn_bq", "L0_xattn_Wk", "L0_xattn_bk",
        "L0_xattn_Wv", "L0_xattn_bv", "L0_xattn_Wo", "L0_xattn_bo", "L0_ffn_Wp", "L0_ffn_sim_matrix",
        "L0_ffn_temperature", "L0_ffn_W1", "L0_ffn_b1", "L0_ffn_W2", "L0_ffn_b2"]


def kernel(**inputs):
    import numpy as _np
    import concourse.bacc as _bacc
    from concourse import mybir as _mybir
    from concourse.bass_utils import run_bass_kernel_spmd as _run

    nc = _bacc.Bacc("TRN2", target_bir_lowering=False, num_devices=1)
    arrays, args = {}, []
    for name in _INS:
        a = _np.ascontiguousarray(inputs[name])
        if a.ndim == 0:
            a = a.reshape(1)
        arrays[f"in_{name}_dram"] = a
        args.append(nc.dram_tensor(f"in_{name}_dram", a.shape, _mybir.dt.from_np(a.dtype), kind="ExternalInput").ap())
    shape = inputs["x"].shape
    args.append(nc.dram_tensor("out_0_dram", shape, _mybir.dt.float32, kind="ExternalOutput").ap())
    layer(nc, *args)
    r = _run(nc, [arrays], core_ids=[0])
    return r.results[0]["out_0_dram"]
```

```python
import math
from contextlib import ExitStack

import concourse.bass as bass
from concourse import mybir

ALU = mybir.AluOpType
ACT = mybir.ActivationFunctionType
AX_X = mybir.AxisListType.X
F32 = mybir.dt.float32
BF16 = mybir.dt.bfloat16
U32 = mybir.dt.uint32

P = 128
LN_EPS = 1e-5
L2_EPS = 1e-12
MASK_SCALE = -1e9
SUM_FLOOR = 1e-36
SUM_LEAST, SUM_MOST = 1e-25, 1e30
PARTS = 3
TERMS = [(0, 0), (0, 1), (0, 2), (1, 0), (1, 1), (2, 0)]
UP_SLOTS = [15, 18, 19, 20, 21, 21, 22, 22]
GELU_SLOTS = [22, 54]
LATE_STEPS = ["oT", "oT", "onT", "wo", "wo", "wo", "wo", "xnT"]
DVE_PARTS = (0,)
DVE_FROM = 2
CHOOSE_SLOTS = [17, 19]
KEYS_SLOT = 22
BOUND_SLOT = 23
NORM_SLOT = 10
COMBINE_SLOT = 23
MIXED_SLOTS = [24, 24, 28, 30, 32, 33, 34, 34, 36, 38, 39, 40, 41, 41, 45, 47]
DOWN_SLOTS = [56, 57, 58, 59, 60, 61, 62, 65]
BUFFERS = 3


def layer(nc, x, ctx_kv, mask, Wq, bq, Wk, bk, Wv, bv, Wo, bo, Wp, sim, temp, W1, b1, W2, b2, out):
    B, S, D = x.shape
    KV = ctx_kv.shape[1]
    E, _, F = W1.shape
    H = 16
    HD = D // H
    HG = 4
    PAIRS = H // 2
    PR = 2 * HD
    CROW = len(TERMS) * PR
    KROWS = CROW + PARTS
    NCH = -(-KV // P)
    KEYS = [min(P, KV - c * P) for c in range(NCH)]
    SLOTS = HG * NCH
    TT = S // P
    NT = B * TT
    FC = F // P
    EF = E * FC
    GW = D + E
    INV_SQRT_D = float(D) ** -0.5
    BANK = 512
    NK4 = -(-NCH // 4)
    NM2 = -(-NCH // 2)
    MB = 3

    before = [("bias", 0, 0)] + [("ctxT", 0, i) for i in range(NK4)] + [("kT", 0, i) for i in range(NK4)] + \
        [("xnT0", 0, i) for i in range(NT // 4)] + [("q", 0, i) for i in range(B * S // BANK)] + \
        [("shift", 0, 0)] + [("v", 0, i) for i in range(NK4)] + [("maskT", 0, i) for i in range(MB)]
    first_batch = [(0, "maskT", 0, 3), (1, "maskT", 0, 4), (2, "maskT", 0, 5), (3, "maskT", 0, 6), (13, "kT", 1, 0),
                   (16, "kT", 1, 1), (19, "kT", 1, 2), (21, "kT", 1, 3), (27, "simT", 0, 0), (29, "WpT", 0, 0),
                   (32, "WpSim", 0, 0)]
    during = [(0, "maskT", 0, 5), (2, "maskT", 0, 6), (3, "v", 0, 1), (3, "v", 0, 2), (3, "v", 0, 3),
              (4, "oT", -1, 3), (5, "ctxT", 1, 0), (6, "onT", -1, 0), (7, "ctxT", 1, 1), (8, "wo", -1, 0),
              (9, "ctxT", 1, 2), (10, "ctxT", 1, 3), (11, "kT", 1, 0), (12, "xnT", -1, 0), (13, "kT", 1, 1),
              (14, "gate", -1, 0), (15, "kT", 1, 3), (16, "kT", 1, 2), (18, "oT", 0, 0), (25, "combT", -1, 0),
              (27, "b2", -1, 0), (29, "shift", 1, 0), (31, "oT", 0, 1), (42, "maskT", 1, 0), (43, "maskT", 1, 1),
              (45, "oT", 0, 2), (46, "maskT", 1, 2), (47, "v", 1, 0), (48, "maskT", 1, 3), (50, "maskT", 1, 4)]
    after = [("oT", B - 1, 3), ("onT", B - 1, 0), ("wo", B - 1, 0), ("xnT", B - 1, 0), ("gate", B - 1, 0),
             ("combT", B - 1, 0), ("b2", B - 1, 0), ("verdict", 0, 0)]
    SCALAR_KINDS = ("ctxT", "kT", "maskT", "onT")

    def by_act(step):
        return step[0] in SCALAR_KINDS

    HALF = E // 2
    UPE = FC // 2
    slot_of = {}
    first_half = [("up", 0, e, i) for e in range(HALF) for i in range(UPE)]
    mixed = [("down", 0, 0, t) for t in range(TT)]
    for e in range(HALF):
        if e + 1 < HALF:
            mixed += [("down", 0, e + 1, t) for t in range(TT)]
        mixed += [("up", 1, e, i) for i in range(UPE)]
    last_half = [("down", 1, e, t) for e in range(HALF) for t in range(TT)]
    for units, slots in ((first_half, UP_SLOTS), (mixed, MIXED_SLOTS), (last_half, DOWN_SLOTS)):
        slot_of.update(zip(units, slots, strict=True))
    order = first_half + mixed + last_half
    place = {unit: n for n, unit in enumerate(order)}

    def units_in(b, slot):
        return [(b - 1 - late, unit) for late in (1, 0) if b - 1 - late >= 0
                for unit in order if slot_of[unit] == slot + late * SLOTS]

    reader = ["down" if u[0] == "down" else
              "pre_dve" if u[3] in DVE_PARTS or (u[1] == 0 and u[2] >= DVE_FROM) else "pre_act" for u in order]
    read_with = [sum(r == reader[n] for r in reader[:n + 1]) for n in range(len(order))]
    per_batch = {r: reader.count(r) for r in ("down", "pre_dve", "pre_act")}

    def read_count(b, unit):
        return b * per_batch[reader[place[unit]]] + read_with[place[unit]]

    b2_slot = next(slot for slot, kind, _, _ in during if kind == "b2")
    downs_before_b2 = sum(u[0] == "down" and slot_of[u] < b2_slot for u in order)
    late_at = {}
    for n, unit in enumerate(u for u in order if slot_of[u] >= SLOTS):
        late_at.setdefault(LATE_STEPS[min(n, len(LATE_STEPS) - 1)], []).append(unit)
    UNITS, DOWNS = len(order), per_batch["down"]

    with ExitStack() as ctx:
        def sb(name, shape, dt=F32):
            return ctx.enter_context(nc.sbuf_tensor(name, shape, dt))

        def psum(name, shape):
            return ctx.enter_context(nc.psum_tensor(name, shape, F32))

        xs = sb("xs", [P, NT, D])
        ctx_nat = sb("ctx_nat", [P, NCH, D])
        mask_nat = sb("mask_nat", [P, MB, TT, 2 * P])
        maskT = sb("maskT", [P, NCH, S])
        ctxT = sb("ctxT", [P, KV])
        kT = sb("kT", [P, KV])
        kpart = [sb(f"kpart{i}", [P, KV], BF16) for i in range(PARTS)]
        kstack_flat = sb("kstack", [KROWS, PAIRS * KV], BF16)
        kstack = kstack_flat[:, :].rearrange("r (p k) -> r p k", p=PAIRS)
        qstack = sb("qstack", [KROWS, B, PAIRS, 2, S], BF16)
        vals = sb("vals", [P, NCH, H, HD + 1])
        masked = sb("masked", [P, BUFFERS, 4 * S])
        probs = sb("probs", [P, BUFFERS, 4 * S])
        w1 = sb("w1", [P, E, F])
        w2 = sb("w2", [P, EF, D])
        wq, wk, wv, wp = (sb(n, [P, D]) for n in ("wq", "wk", "wv", "wp"))
        wo = sb("wo", [P, D])
        bv_all, bo_all = sb("bv_all", [P, D]), sb("bo_all", [P, D])
        bias_rows = sb("bias_rows", [EF + 2, D])
        bias_cols = sb("bias_cols", [P, EF + 2])
        b2_rows = sb("b2_rows", [E, D])
        sim_rows = sb("sim_rows", [E, D])
        simT = sb("simT", [P, E])
        tiny = sb("tiny", [P, 16])
        wg = sb("wg", [P, GW])
        ident = sb("ident", [P, P])
        blk = sb("blk", [P, H])
        negblk = sb("negblk", [P, H])
        half = sb("half", [P, 2])
        minus_half = sb("minus_half", [P, NT])
        iota8 = sb("iota8", [P, E])
        stats = sb("stats", [P, NT, 6])
        moments = sb("moments", [P, NT, 2])
        var_eps = sb("var_eps", [P, NT])
        rstd = sb("rstd", [P, NT])
        qabs = sb("qabs", [P, B * S], BF16)
        kmax = sb("kmax", [P, 1])
        ub = sb("ub", [P, S])
        shift = sb("shift", [H, S])
        shift_part = [sb(f"shift_part{i}", [H, S], BF16) for i in range(PARTS)]
        osum = sb("osum", [P, S])
        onat = sb("onat", [P, TT, H, HD])
        onT = osum
        xn2 = onat[:, :, :, :].rearrange("p t h d -> p t (h d)")
        xn2T = sb("xn2T", [P, S])
        graw = sb("graw", [P, TT, E])
        gsc = sb("gsc", [P, TT, E])
        sumsq = sb("sumsq", [P, TT])
        rnorm = sb("rnorm", [P, TT])
        junk = sb("junk", [P, D])
        top = sb("top", [P, TT, 8])
        topi = sb("topi", [P, TT, 8], U32)
        topf = sb("topf", [P, TT, 8])
        diff = sb("diff", [P, TT])
        ediff = sb("ediff", [P, TT])
        euler = sb("euler", [P, TT])
        den = sb("den", [P, TT])
        p1, p2 = sb("p1", [P, TT]), sb("p2", [P, TT])
        comb = sb("comb", [P, TT, E])
        hot = sb("hot", [P, E])
        combT = sb("combT", [E, S])
        inverses = sb("inverses", [P, B * HG, TT, 4])
        fine = sb("fine", [P, 2])
        verdict = sb("verdict", [1, 4], mybir.dt.int32)
        top_score = sb("top_score", [P, 2, 8])
        hid = sb("hid", [P, HALF * FC, S])
        flat = hid[:, :, :].rearrange("p a s -> p (a s)")
        xn1 = flat[:, 0:NT * D]
        xn1T = flat[:, NT * D:NT * D + B * S]
        qrest = xn1
        flat16 = flat.bitcast(BF16)
        qpart = [flat16[:, (4 + i) * B * S:(5 + i) * B * S] for i in range(PARTS)]
        w2_16 = w2[:, :, :].rearrange("p a d -> p (a d)").bitcast(BF16)
        qhalf = [w2_16[:, 2 * i * B * S:2 * (i + 1) * B * S].rearrange("p (b a s) -> p b a s", b=B, a=2)
                 for i in range(PARTS)]
        qs = w2[:, :, :].rearrange("p a d -> p (a d)")[:, EF * D - B * S:EF * D]

        score = [psum(f"score{i}", [P, 4 * S]) for i in range(2)]
        pv = psum("pv", [P, BANK])
        misc = psum("misc", [P, BANK])
        ffn = [psum(f"ffn{i}", [P, BANK]) for i in range(2)]
        free = [misc, ffn[0], ffn[1]] + [score[i][:, j * BANK:(j + 1) * BANK] for i in range(2) for j in range(2)]

        def bank_of(n):
            return free[n % len(free)] if n < len(before) else misc

        def used_before(n):
            if n < len(before):
                return n - len(free) if n >= len(free) else None
            return n - 1

        def attempt(ctx, exact):
            NB = BUFFERS - 1 if exact else BUFFERS
            LAG = NB
            top_rows = masked[:, BUFFERS - 1, :]

            steps = list(before)
            at_slot = {(b, slot): [] for b in range(B) for slot in range(SLOTS)}
            for b in range(B):
                own = {(kind, b + rel, part) for _, kind, rel, part in first_batch} if b == 0 else set()
                planned = (first_batch if b == 0 else []) + [s for s in during if (s[1], b + s[2], s[3]) not in own]
                if exact:
                    planned = [(0 if s[1] == "maskT" and s[2] == 0 else s[0],) + s[1:] for s in planned]
                for slot, kind, rel, part in sorted(planned):
                    if 0 <= b + rel < B and (kind, b + rel, part) not in before:
                        at_slot[b, slot].append((len(steps), kind, b + rel, part))
                        steps.append((kind, b + rel, part))
            first_after = len(steps)
            steps += after
            number = {s: n for n, s in enumerate(steps)}
            by_scalar = [sum(map(by_act, steps[:n + 1])) for n in range(len(steps))]
            by_vector = [n + 1 - by_scalar[n] for n in range(len(steps))]

            def sem(name):
                return ctx.enter_context(nc.semaphore(name + ("_exact" if exact else "")))

            x_in, w_in, ctx_in, w1_in, w2_in = (sem(n) for n in ("x_in", "w_in", "ctx_in", "w1_in", "w2_in"))
            mask_in = [sem(f"mask_in{i}") for i in range(MB)]
            k_in, q_in = sem("k_in"), sem("q_in")
            kcopy_done, krest_done, qsplit_done = sem("kcopy_done"), sem("krest_done"), sem("qsplit_done")
            ks_in = [sem(f"ks_in{i}") for i in range(HG)]
            qs_in = [sem(f"qs_in{i}") for i in range(HG)]
            shift_in = sem("shift_in")
            out_done = sem("out_done")
            consts = sem("consts")
            pool_step = sem("pool_step")
            dve_step = sem("dve_step")
            zeroed = sem("zeroed")
            misc_full = sem("misc_full")
            act_took = sem("act_took")
            dve_took = sem("dve_took")
            scored = sem("scored")
            masked_done = sem("masked_done")
            exp_done = sem("exp_done")
            pv_done = sem("pv_done")
            pv_taken = sem("pv_taken")
            ve_ready = sem("ve_ready")
            rstd_ready = sem("rstd_ready")
            xn1_ready = sem("xn1_ready")
            kstat_done = sem("kstat_done")
            ksplit_done = sem("ksplit_done")
            qhalf_ready = sem("qhalf_ready")
            ub_ready = sem("ub_ready")
            qabs_done = sem("qabs_done")
            bo_added = sem("bo_added")
            shift_ready = sem("shift_ready")
            xn2_ready = sem("xn2_ready")
            sq_done = sem("sq_done")
            sq_pool = sem("sq_pool")
            rnorm_ready = sem("rnorm_ready")
            diff_ready = sem("diff_ready")
            ediff_ready = sem("ediff_ready")
            comb_ready = sem("comb_ready")
            ffn_full = sem("ffn_full")
            pre_dve, pre_act = sem("pre_dve"), sem("pre_act")
            gelu_done = sem("gelu_done")
            down_taken = sem("down_taken")
            read_out = {"down": down_taken, "pre_dve": pre_dve, "pre_act": pre_act}
            result_ready = sem("result_ready")
            sn_ready = sem("sn_ready")
            rsim_ready = sem("rsim_ready")
            fine_ready = sem("fine_ready")

            top_scored, top_masked = sem("top_scored"), sem("top_masked")
            top_turned, top_reduced = sem("top_turned"), sem("top_reduced")
            top_spread, top_back, top_taken = sem("top_spread"), sem("top_back"), sem("top_taken")

            block = ctx.enter_context(nc.Block())

            def wait_for_pre(engine, b, unit):
                engine.wait_ge(ffn_full, b * UNITS + place[unit] + 1)
                _, h, e, _ = unit
                if h == 1:
                    engine.wait_ge(ffn_full, b * UNITS + place["down", 0, e, TT - 1] + 1)
                elif b > 0:
                    engine.wait_ge(ffn_full, (b - 1) * UNITS + place["down", 1, e, TT - 1] + 1)

            def rows(a, rep):
                return bass.AP(a.tensor, a.offset, [[0, rep]] + [list(d) for d in a.ap])

            @block.sync
            def _(sp):
                def load_ctx(b):
                    full = (NCH - 1) * P
                    if b > 0:
                        sp.wait_ge(misc_full, number["ctxT", b - 1, NK4 - 1] + 1)
                    sp.dma_start(ctx_nat[:, 0:NCH - 1, :],
                                 ctx_kv[b, 0:full, :].rearrange("(c p) d -> p c d", p=P)).then_inc(ctx_in, 16)
                    sp.dma_start(ctx_nat[0:KEYS[-1], NCH - 1, :], ctx_kv[b, full:KV, :]).then_inc(ctx_in, 16)

                def load_mask(b, i0, i1):
                    for i in range(i0, i1):
                        n = b * NM2 + i
                        if n >= MB:
                            sp.wait_ge(misc_full, number["maskT", (n - MB) // NM2, (n - MB) % NM2] + 1)
                        k0, k1 = 2 * i * P, min(2 * (i + 1) * P, KV)
                        sp.dma_start(mask_nat[:, n % MB, :, 0:k1 - k0],
                                     mask[b, 0].rearrange("(t p) k -> p t k", p=P)[:, :, k0:k1]
                                     ).then_inc(mask_in[n % MB], 16)

                def stack_keys(b, hg):
                    if b > 0 or hg > 0:
                        sp.wait_ge(ksplit_done, b + 1)
                    if b > 0:
                        sp.wait_ge(scored, (b - 1) * SLOTS + (hg + 1) * NCH)
                    for t, (kp, _) in enumerate(TERMS):
                        if b == 0 and hg == 0:
                            sp.wait_ge(*((kcopy_done, kp + 1) if kp < PARTS - 1 else (ksplit_done, 1)))
                        for pair in (2 * hg, 2 * hg + 1):
                            sp.dma_start(kstack[t * PR:(t + 1) * PR, pair, :],
                                         kpart[kp][pair * PR:(pair + 1) * PR, :]).then_inc(ks_in[hg], 16)

                def place_shift(b):
                    sp.wait_ge(shift_ready, b + 1)
                    for i in range(PARTS):
                        sp.dma_start(qstack[CROW + i:CROW + i + 1, b].rearrange("o p a s -> o (p a) s"),
                                     shift_part[i][:, :]).then_inc(shift_in, 16)

                load_ctx(0)
                sp.dma_start(wk[:, :], Wk).then_inc(k_in, 16)
                sp.dma_start(bias_rows[0:EF, :], b1.rearrange("e (c p) -> (e c) p", p=P)).then_inc(k_in, 16)
                sp.dma_start(bias_rows[EF:EF + 1, :], rows(bq, 1)).then_inc(k_in, 16)
                sp.dma_start(bias_rows[EF + 1:EF + 2, :], rows(bk, 1)).then_inc(k_in, 16)
                load_mask(0, 0, MB)
                stack_keys(0, 0)
                place_shift(0)
                load_mask(0, MB, NM2)
                load_ctx(1)
                stack_keys(0, 1)
                stack_keys(0, 2)
                stack_keys(0, 3)
                for b in range(B):
                    if b == 0:
                        sp.dma_start(w1[:, :, :], W1.rearrange("e d f -> d e f")).then_inc(w1_in, 16)
                        for hg in range(HG):
                            sp.wait_ge(qs_in[hg], 16 * 2 * len(TERMS))
                        sp.wait_ge(qabs_done, 1)
                        sp.dma_start(w2[:, :, :], W2.rearrange("e (c p) d -> p (e c) d", p=P)).then_inc(w2_in, 16)
                    if b + 1 < B:
                        load_mask(b + 1, 0, MB)
                        stack_keys(b + 1, 0)
                        if b + 2 < B:
                            load_ctx(b + 2)
                        place_shift(b + 1)
                        load_mask(b + 1, MB, NM2)
                        stack_keys(b + 1, 1)
                        stack_keys(b + 1, 2)
                        stack_keys(b + 1, 3)
                    if b > 0:
                        sp.wait_ge(result_ready, b)
                        sp.dma_start(out[b - 1].rearrange("(t p) d -> p t d", p=P),
                                     xs[:, (b - 1) * TT:b * TT, :]).then_inc(out_done, 16)
                sp.wait_ge(result_ready, B)
                sp.dma_start(out[B - 1].rearrange("(t p) d -> p t d", p=P), xs[:, (B - 1) * TT:, :]).then_inc(out_done, 16)
                sp.wait_ge(out_done, 16 * B)

            @block.gpsimd
            def _(pool):
                chain = [0]

                def link(ins):
                    chain[0] += 1
                    ins.then_inc(pool_step, 1)
                    pool.wait_ge(pool_step, chain[0])

                link(nc.gpsimd.memset(ident[:, :], 0.0))
                nc.gpsimd.affine_select(out=ident[:, :], in_=ident[:, :], compare_op=ALU.not_equal, fill=1.0, base=0,
                                        pattern=[[-1, P]], channel_multiplier=1).then_inc(consts, 1)
                link(nc.gpsimd.memset(minus_half[:, :], -0.5))
                link(nc.gpsimd.memset(euler[:, :], math.e))
                nc.gpsimd.memset(kstack_flat[CROW:KROWS, :].bitcast(U32),
                                 0x3F803F80).then_inc(consts, 1)
                pool.wait_ge(consts, 2)
                link(nc.gpsimd.memset(blk[:, :], 1.0))
                link(nc.gpsimd.affine_select(out=blk[:, :], in_=blk[:, :], compare_op=ALU.is_ge, fill=0.0, base=0,
                                             pattern=[[-HD, H]], channel_multiplier=1))
                nc.gpsimd.affine_select(out=blk[:, :], in_=blk[:, :], compare_op=ALU.is_ge, fill=0.0, base=HD - 1,
                                        pattern=[[HD, H]], channel_multiplier=-1).then_inc(consts, 1)
                nc.gpsimd.iota(iota8[:, :], pattern=[[1, E]], base=0, channel_multiplier=0,
                               allow_small_or_imprecise_dtypes=True).then_inc(consts, 1)
                pool.wait_ge(ve_ready, 1)
                nc.gpsimd.tensor_tensor(rstd[:, :], var_eps[:, :], minus_half[:, :], ALU.pow).then_inc(rstd_ready, 1)

                def split_keys(b):
                    pool.wait_ge(act_took, by_scalar[number["kT", b, NK4 - 1]])
                    if b > 0:
                        pool.wait_ge(ks_in[HG - 1], 16 * 2 * len(TERMS) * b)
                    link(nc.gpsimd.tensor_copy(kpart[0][:, :], kT[:, :]))
                    pool.wait_ge(kstat_done, b + 1)
                    link(nc.gpsimd.tensor_tensor(kT[:, :], kT[:, :], kpart[0][:, :], ALU.subtract))
                    link(nc.gpsimd.tensor_copy(kpart[1][:, :], kT[:, :]))
                    nc.gpsimd.tensor_tensor(kpart[2][:, :], kT[:, :], kpart[1][:, :],
                                            ALU.subtract).then_inc(ksplit_done, 1)

                def split_shift(b):
                    pool.wait_ge(dve_took, by_vector[number["shift", b, 0]])
                    pool.wait_ge(shift_in, 16 * PARTS * b)
                    link(nc.gpsimd.tensor_copy(shift_part[0][:, :], shift[:, :]))
                    link(nc.gpsimd.tensor_tensor(shift[:, :], shift[:, :], shift_part[0][:, :], ALU.subtract))
                    link(nc.gpsimd.tensor_copy(shift_part[1][:, :], shift[:, :]))
                    nc.gpsimd.tensor_tensor(shift_part[2][:, :], shift[:, :], shift_part[1][:, :],
                                            ALU.subtract).then_inc(shift_ready, 1)

                for hg in range(HG):
                    for qp, t in sorted((qp, t) for t, (_, qp) in enumerate(TERMS)):
                        pool.wait_ge(qhalf_ready, 2 * (qp + 1))
                        for pair in (2 * hg, 2 * hg + 1):
                            pool.dma_start(qstack[t * PR:(t + 1) * PR, :, pair],
                                           qhalf[qp][pair * PR:(pair + 1) * PR]).then_inc(qs_in[hg], 16)
                bov = bass.AP(bo_all[:, :].tensor, bo_all[:, :].offset,
                              [list(bo_all[:, :].ap[0]), [0, NT], [1, D]])
                pool.wait_ge(xn1_ready, NT)
                pool.wait_ge(w_in, 16 * 8)
                nc.gpsimd.tensor_tensor(xs[:, :, :], xs[:, :, :], bov, ALU.add).then_inc(bo_added, 1)
                pool.wait_ge(sq_pool, 1)
                nc.gpsimd.tensor_tensor(tiny[0:E, 3:4], tiny[0:E, 2:3], minus_half[0:E, 0:1],
                                        ALU.pow).then_inc(rsim_ready, 1)
                for b in range(B + 1):
                    if b > 0:
                        pool.wait_ge(ve_ready, b + 1)
                        nc.gpsimd.tensor_tensor(rstd[:, 0:TT], var_eps[:, 0:TT], minus_half[:, 0:TT],
                                                ALU.pow).then_inc(rstd_ready, 1)
                    if b > 0:
                        pool.wait_ge(sq_pool, b + 1)
                        nc.gpsimd.tensor_tensor(rnorm[:, :], sumsq[:, :], minus_half[:, 0:TT],
                                                ALU.pow).then_inc(rnorm_ready, 1)
                        pool.wait_ge(diff_ready, b)
                        nc.gpsimd.tensor_tensor(ediff[:, :], euler[:, :], diff[:, :],
                                                ALU.pow).then_inc(ediff_ready, 1)
                    if b + 1 < B:
                        split_keys(b + 1)
                        split_shift(b + 1)

            @block.tensor
            def _(pe):
                def misc_step(n, kind, b, i):
                    m = used_before(n)
                    if m is not None:
                        if by_act(steps[m]):
                            pe.wait_ge(act_took, by_scalar[m])
                        else:
                            pe.wait_ge(dve_took, by_vector[m])
                    misc = bank_of(n)
                    last = None
                    if kind == "bias":
                        pe.wait_ge(k_in, 16 * 4)
                        pe.wait_ge(consts, 2)
                        last = nc.tensor.transpose(misc[:, 0:EF + 2], bias_rows[:, :], ident[0:EF + 2, 0:EF + 2])
                    elif kind == "xnT0":
                        pe.wait_ge(xn1_ready, 4 * (i + 1))
                        for j in range(4):
                            c = 4 * i + j
                            last = nc.tensor.transpose(misc[:, j * P:(j + 1) * P], xn1[:, c * D:(c + 1) * D], ident[:, :])
                    elif kind == "q":
                        pe.wait_ge(q_in, 16)
                        pe.wait_ge(dve_took, by_vector[number["xnT0", 0, i]])
                        last = nc.tensor.matmul(misc[:, :], wq[:, :], xn1T[:, i * BANK:(i + 1) * BANK],
                                                start=True, stop=True)
                    elif kind == "ctxT":
                        pe.wait_ge(ctx_in, 32 * (b + 1))
                        for j, c in enumerate(range(4 * i, min(4 * i + 4, NCH))):
                            k = KEYS[c]
                            last = nc.tensor.transpose(misc[:, j * P:j * P + k], ctx_nat[0:k, c, :], ident[0:k, 0:k])
                    elif kind == "kT":
                        pe.wait_ge(act_took, by_scalar[number["ctxT", b, NK4 - 1]])
                        k0, k1 = i * BANK, min((i + 1) * BANK, KV)
                        last = nc.tensor.matmul(misc[:, 0:k1 - k0], wk[:, :], ctxT[:, k0:k1], start=True, stop=True)
                    elif kind == "v":
                        if b == 0:
                            pe.wait_ge(w_in, 16 * 8)
                        pe.wait_ge(act_took, by_scalar[number["ctxT", b, NK4 - 1]])
                        for j, c in enumerate(range(4 * i, min(4 * i + 4, NCH))):
                            k = KEYS[c]
                            last = nc.tensor.matmul(misc[0:k, j * P:(j + 1) * P], ctxT[:, c * P:c * P + k], wv[:, :],
                                                    start=True, stop=True)
                    elif kind == "maskT":
                        n4 = b * NM2 + i
                        pe.wait_ge(mask_in[n4 % MB], 16 * (n4 // MB + 1))
                        for j, c in enumerate(range(2 * i, min(2 * i + 2, NCH))):
                            k = KEYS[c]
                            for t in range(TT):
                                at = j * S + t * P
                                last = nc.tensor.transpose(misc[0:k, at:at + P], mask_nat[:, n4 % MB, t, j * P:j * P + k],
                                                           ident[:, :])
                    elif kind == "shift":
                        pe.wait_ge(ub_ready, b + 1)
                        last = nc.tensor.matmul(misc[0:H, 0:S], negblk[:, :], ub[:, :], start=True, stop=True)
                    elif kind == "simT":
                        pe.wait_ge(sn_ready, 1)
                        last = nc.tensor.transpose(misc[:, 0:E], sim_rows[:, :], ident[0:E, 0:E])
                    elif kind == "WpT":
                        last = nc.tensor.transpose(misc[:, 0:D], wp[:, :], ident[:, :])
                    elif kind == "WpSim":
                        pe.wait_ge(dve_took, by_vector[number["simT", 0, 0]])
                        last = nc.tensor.matmul(misc[:, 0:E], wp[:, :], simT[:, :], start=True, stop=True)
                    elif kind == "oT":
                        pe.wait_ge(pv_taken, b * HG + i + 1)
                        for t in range(TT):
                            last = nc.tensor.transpose(misc[:, t * P:(t + 1) * P], osum[:, t * P:(t + 1) * P], ident[:, :])
                    elif kind == "verdict":
                        pe.wait_ge(fine_ready, 1)
                        last = nc.tensor.transpose(misc[0:1, 0:P], fine[:, 0:1], ident[:, :])
                    elif kind == "onT":
                        pe.wait_ge(dve_took, by_vector[number["oT", b, HG - 1]])
                        for t in range(TT):
                            last = nc.tensor.transpose(misc[:, t * P:(t + 1) * P],
                                                       onat[:, t].rearrange("p h d -> p (h d)"), ident[:, :])
                    elif kind == "wo":
                        pe.wait_ge(act_took, by_scalar[number["onT", b, 0]])
                        for t in range(TT):
                            last = nc.tensor.matmul(misc[:, t * D:(t + 1) * D], onT[:, t * P:(t + 1) * P], wo[:, :],
                                                    start=True, stop=True)
                    elif kind == "xnT":
                        pe.wait_ge(xn2_ready, b + 1)
                        for t in range(TT):
                            last = nc.tensor.transpose(misc[:, t * P:(t + 1) * P], xn2[:, t, :], ident[:, :])
                    elif kind == "gate":
                        pe.wait_ge(dve_took, by_vector[number["xnT", b, 0]])
                        for t in range(TT):
                            last = nc.tensor.matmul(misc[:, t * GW:(t + 1) * GW], xn2T[:, t * P:(t + 1) * P], wg[:, :],
                                                    start=True, stop=True)
                    elif kind == "combT":
                        pe.wait_ge(comb_ready, b + 1)
                        for t in range(TT):
                            last = nc.tensor.transpose(misc[0:E, t * P:(t + 1) * P], comb[:, t, :], ident[:, :])
                    elif kind == "b2":
                        pe.wait_ge(dve_took, by_vector[number["combT", b, 0]])
                        for t in range(TT):
                            last = nc.tensor.matmul(misc[:, t * D:(t + 1) * D], combT[:, t * P:(t + 1) * P],
                                                    b2_rows[:, :], start=True, stop=True)
                    last.then_inc(misc_full, 1)

                def stacked(b, hg):
                    pe.wait_ge(ks_in[hg], 16 * 2 * len(TERMS) * (b + 1))
                    if b == 0:
                        pe.wait_ge(qs_in[hg], 16 * 2 * len(TERMS))
                    if hg == 0:
                        pe.wait_ge(shift_in, 16 * PARTS * (b + 1))

                def products(b, hg, ch, to):
                    k = KEYS[ch]
                    for j in range(2):
                        pair = 2 * hg + j
                        last = nc.tensor.matmul(to[0:k, j * BANK:(j + 1) * BANK],
                                                kstack[:, pair, ch * P:ch * P + k],
                                                qstack[:, b, pair].rearrange("r a s -> r (a s)"),
                                                start=True, stop=True)
                    return last

                def scores(b, hg, ch):
                    g = b * SLOTS + hg * NCH + ch
                    if ch == 0:
                        stacked(b, hg)
                    if g >= 2:
                        pe.wait_ge(masked_done, g - 1)
                    if exact and ch == 0:
                        pe.wait_ge(top_taken, b * HG + hg + 1)
                    products(b, hg, ch, score[g % 2]).then_inc(scored, 1)

                def largest(b, hg):
                    hgn = b * HG + hg
                    stacked(b, hg)
                    if hgn > 0:
                        pe.wait_ge(masked_done, hgn * NCH)
                    for ch in range(NCH):
                        n = hgn * NCH + ch
                        products(b, hg, ch, score[0]).then_inc(top_scored, 1)
                        pe.wait_ge(top_masked, n + 1)
                        k = KEYS[ch]
                        for j in range(2 * 4):
                            last = nc.tensor.transpose(score[1][:, j * P:j * P + k],
                                                       masked[0:k, 0, j * P:(j + 1) * P], ident[0:k, 0:k])
                        last.then_inc(top_turned, 1)
                        pe.wait_ge(top_reduced, n + 1)
                    pe.wait_ge(top_spread, hgn + 1)
                    for j in range(2 * 4):
                        last = nc.tensor.transpose(score[1][:, j * P:(j + 1) * P], masked[:, 0, j * P:(j + 1) * P],
                                                   ident[:, :])
                    last.then_inc(top_back, 1)

                def values(g):
                    b, hg, ch = g // SLOTS, g % SLOTS // NCH, g % NCH
                    if ch == 0 and g > 0:
                        pe.wait_ge(pv_taken, g // NCH)
                    pe.wait_ge(exp_done, g + 1)
                    k = KEYS[ch]
                    for j in range(4):
                        last = nc.tensor.matmul(pv[32 * j:32 * j + HD + 1, 0:S], vals[0:k, ch, 4 * hg + j, :],
                                                probs[0:k, g % NB, j * S:(j + 1) * S], start=(ch == 0),
                                                stop=(ch == NCH - 1), tile_position=(0, 32 * j))
                    last.then_inc(pv_done, 1)

                def ffn_unit(b, unit):
                    kind, h, e, part = unit
                    n = b * UNITS + place[unit]
                    if n >= 2:
                        was = order[(n - 2) % UNITS]
                        pe.wait_ge(read_out[reader[place[was]]], read_count((n - 2) // UNITS, was))
                    bank = ffn[n % 2]
                    if kind == "up":
                        if n == 0:
                            pe.wait_ge(w1_in, 16)
                        for j in range(2):
                            c = 2 * part + j
                            last = nc.tensor.matmul(bank[:, j * S:(j + 1) * S],
                                                    w1[:, h * HALF + e, c * P:(c + 1) * P], xn2T[:, :],
                                                    start=True, stop=True)
                    else:
                        if part == 0:
                            pe.wait_ge(gelu_done, (2 * b + h) * HALF + e + 1)
                        if b == 0 and h == 0 and e == 0:
                            pe.wait_ge(w2_in, 16)
                        for c in range(FC):
                            last = nc.tensor.matmul(bank[:, 0:D], hid[:, e * FC + c, part * P:(part + 1) * P],
                                                    w2[:, (h * HALF + e) * FC + c, :], start=(c == 0),
                                                    stop=(c == FC - 1))
                    last.then_inc(ffn_full, 1)

                for n, (kind, b, i) in enumerate(before):
                    misc_step(n, kind, b, i)
                    pe.wait_ge(zeroed, 1)
                pe.wait_ge(act_took, by_scalar[len(before) - 1])
                pe.wait_ge(dve_took, by_vector[len(before) - 1])
                for b in range(B):
                    for slot in range(SLOTS):
                        g = b * SLOTS + slot
                        for step in at_slot[b, slot]:
                            misc_step(*step)
                        if exact and slot % NCH == 0:
                            largest(b, slot // NCH)
                        scores(b, slot // NCH, slot % NCH)
                        if g >= LAG:
                            values(g - LAG)
                        for fb, unit in units_in(b, slot):
                            ffn_unit(fb, unit)
                for g in range(B * SLOTS - LAG, B * SLOTS):
                    values(g)
                for n in range(first_after, len(steps) - 1):
                    if steps[n][0] == "combT":
                        for unit in mixed[:2]:
                            ffn_unit(B - 1, unit)
                    misc_step(n, *steps[n])
                    for unit in late_at.get(steps[n][0], []):
                        ffn_unit(B - 2, unit)
                    if steps[n][0] == "gate":
                        for unit in first_half:
                            ffn_unit(B - 1, unit)
                for unit in mixed[2:] + last_half:
                    ffn_unit(B - 1, unit)
                misc_step(len(steps) - 1, *steps[-1])

            @block.scalar
            def _(act):
                def misc_step(n, kind, b, i):
                    misc = bank_of(n)
                    if by_act((kind, b, i)):
                        act.wait_ge(misc_full, n + 1)
                    if kind == "ctxT":
                        if b > 0 and i == 0:
                            act.wait_ge(misc_full, number["v", b - 1, NK4 - 1] + 1)
                        k0, k1 = i * BANK, min((i + 1) * BANK, KV)
                        nc.scalar.activation(ctxT[:, k0:k1], misc[:, 0:k1 - k0], ACT.Copy).then_inc(act_took, 1)
                    elif kind == "kT":
                        if i == 0 and b == 0:
                            act.wait_ge(dve_took, 1)
                        elif i == 0:
                            act.wait_ge(ksplit_done, b)
                        k0, k1 = i * BANK, min((i + 1) * BANK, KV)
                        nc.scalar.activation(kT[:, k0:k1], misc[:, 0:k1 - k0], ACT.Identity,
                                             bias=bias_cols[:, EF + 1:EF + 2]).then_inc(act_took, 1)
                    elif kind == "maskT":
                        c0, c1 = 2 * i, min(2 * i + 2, NCH)
                        if b > 0:
                            act.wait_ge(masked_done, b * SLOTS - NCH + c1)
                        k = KEYS[c1 - 1]
                        nc.scalar.activation(maskT[0:k, c0:c1, :].rearrange("p c s -> p (c s)"),
                                             misc[0:k, 0:(c1 - c0) * S], ACT.Copy, scale=MASK_SCALE).then_inc(act_took, 1)
                    elif kind == "onT":
                        nc.scalar.activation(onT[:, :], misc[:, 0:S], ACT.Copy).then_inc(act_took, 1)
                    elif kind == "gate":
                        act.wait_ge(misc_full, n + 1)
                        for t in range(TT):
                            nc.scalar.activation(junk[:, :], misc[:, t * GW:t * GW + D], ACT.Square,
                                                 accum_out=sumsq[:, t:t + 1]).then_inc(sq_done, 1)
                            act.wait_ge(sq_done, b * TT + t + 1)

                def exps(g):
                    k = KEYS[g % NCH]
                    act.wait_ge(masked_done, g + 1)
                    if g >= NB:
                        act.wait_ge(pv_done, g - NB + 1)
                    nc.scalar.activation(probs[0:k, g % NB, :], masked[0:k, g % NB, :], ACT.Exp).then_inc(exp_done, 1)

                def hidden(b, unit):
                    _, h, e, part = unit
                    wait_for_pre(act, b, unit)
                    for j in range(2):
                        c = e * FC + 2 * part + j
                        k = h * HALF * FC + c
                        last = nc.scalar.activation(hid[:, c, :],
                                                    ffn[(b * UNITS + place[unit]) % 2][:, j * S:(j + 1) * S],
                                                    ACT.Identity, bias=bias_cols[:, k:k + 1])
                    last.then_inc(pre_act, 1)

                def gelu(b, h, e):
                    for part in range(UPE):
                        unit = ("up", h, e, part)
                        act.wait_ge(read_out[reader[place[unit]]], read_count(b, unit))
                    layer_e = hid[:, e * FC:(e + 1) * FC, :].rearrange("p c s -> p (c s)")
                    nc.scalar.activation(layer_e, layer_e, ACT.Gelu).then_inc(gelu_done, 1)

                act.dma_start(xs[:, :, :], x.rearrange("b (t p) d -> p (b t) d", p=P)).then_inc(x_in, 16)
                act.dma_start(wq[:, :], Wq).then_inc(q_in, 16)
                for dst, src in ((wv[:, :], Wv), (bv_all[:, :], rows(bv, P)), (bo_all[:, :], rows(bo, P)),
                                 (b2_rows[:, :], b2), (sim_rows[:, :], sim), (wp[:, :], Wp), (wo[:, :], Wo),
                                 (tiny[:, 0:1], bass.AP(temp.tensor, temp.offset, [[0, P], [1, 1]]))):
                    act.dma_start(dst, src).then_inc(w_in, 16)
                for n, (kind, b, i) in enumerate(before):
                    misc_step(n, kind, b, i)
                    if kind == "kT" and i == NK4 - 1:
                        act.wait_ge(act_took, by_scalar[n])
                        nc.scalar.activation(kpart[0][:, :], kT[:, :], ACT.Copy).then_inc(kcopy_done, 1)
                    if kind == "q" and i == B * S // BANK - 1:
                        for part in range(PARTS):
                            act.wait_ge(qsplit_done, part + 1)
                            for a in range(2):
                                nc.scalar.activation(qhalf[part][:, :, a, :],
                                                     qpart[part].rearrange("p (b s) -> p b s", b=B), ACT.Copy,
                                                     scale=half[:, a:a + 1]).then_inc(qhalf_ready, 1)
                    if kind == "shift":
                        act.wait_ge(krest_done, 1)
                        nc.scalar.activation(kpart[1][:, :], kT[:, :], ACT.Copy).then_inc(kcopy_done, 1)
                for b in range(B):
                    for slot in range(SLOTS):
                        for step in at_slot[b, slot]:
                            misc_step(*step)
                        if b * SLOTS + slot > 0:
                            exps(b * SLOTS + slot - 1)
                        for fb, unit in units_in(b, slot):
                            if reader[place[unit]] == "pre_act":
                                hidden(fb, unit)
                        for h, gelu_slot in enumerate(GELU_SLOTS):
                            fb = b - 1 - gelu_slot // SLOTS
                            if slot == gelu_slot % SLOTS and fb >= 0:
                                for e in range(HALF):
                                    gelu(fb, h, e)
                exps(B * SLOTS - 1)
                if GELU_SLOTS[1] >= SLOTS:
                    for e in range(HALF):
                        gelu(B - 2, 1, e)
                for n in range(first_after, len(steps)):
                    misc_step(n, *steps[n])
                for h, units in enumerate((first_half, mixed)):
                    for unit in units:
                        if reader[place[unit]] == "pre_act":
                            hidden(B - 1, unit)
                        if unit[0] == "up" and unit[3] == UPE - 1:
                            gelu(B - 1, unit[1], unit[2])

            @block.vector
            def _(dve):
                chain = [0]

                def link(ins):
                    chain[0] += 1
                    ins.then_inc(dve_step, 1)
                    dve.wait_ge(dve_step, chain[0])

                def moments_of(tile, n):
                    link(nc.vector.bn_stats(stats[:, n, :], tile))
                    link(nc.vector.bn_aggr(moments[:, n, :], stats[:, n, :]))

                def split_keys_first():
                    dve.wait_ge(kcopy_done, 1)
                    dve.wait_ge(kstat_done, 1)
                    nc.vector.tensor_tensor(kT[:, :], kT[:, :], kpart[0][:, :], ALU.subtract).then_inc(krest_done, 1)
                    bound(0)
                    dve.wait_ge(kcopy_done, 2)
                    nc.vector.tensor_tensor(kpart[2][:, :], kT[:, :], kpart[1][:, :],
                                            ALU.subtract).then_inc(ksplit_done, 1)

                def key_extremes(b):
                    dve.wait_ge(act_took, by_scalar[number["kT", b, NK4 - 1]])
                    nc.vector.tensor_reduce(kmax[:, :], kT[:, :], AX_X, ALU.max,
                                            apply_absolute_value=True).then_inc(kstat_done, 1)

                def bound(b):
                    dve.wait_ge(kstat_done, b + 1)
                    dve.wait_ge(qabs_done, 1)
                    nc.vector.tensor_scalar(ub[:, :], qabs[:, b * S:(b + 1) * S], kmax[:, :], None,
                                            ALU.mult).then_inc(ub_ready, 1)

                def misc_step(n, kind, b, i):
                    if by_act((kind, b, i)):
                        return
                    misc = bank_of(n)
                    dve.wait_ge(misc_full, n + 1)
                    if kind == "verdict":
                        nc.vector.tensor_reduce(fine[0:1, 1:2], misc[0:1, 0:P], AX_X, ALU.min).then_inc(dve_took, 1)
                        dve.wait_ge(dve_took, by_vector[n])
                        link(nc.vector.tensor_scalar(verdict[:, 0:1], fine[0:1, 1:2], 0.5, None, ALU.is_lt))
                    elif kind == "bias":
                        nc.vector.tensor_copy(bias_cols[:, :], misc[:, 0:EF + 2]).then_inc(dve_took, 1)
                    elif kind == "xnT0":
                        nc.vector.tensor_copy(xn1T[:, i * BANK:(i + 1) * BANK], misc[:, :]).then_inc(dve_took, 1)
                    elif kind == "q":
                        if i == 0:
                            dve.wait_ge(dve_took, 1)
                        sl = slice(i * BANK, (i + 1) * BANK)
                        nc.vector.tensor_scalar(qs[:, sl], misc[:, :], bias_cols[:, EF:EF + 1], INV_SQRT_D, ALU.add,
                                                ALU.mult).then_inc(dve_took, 1)
                        if i == B * S // BANK - 1:
                            dve.wait_ge(dve_took, by_vector[n])
                            nc.vector.tensor_copy(qpart[0], qs[:, :]).then_inc(qsplit_done, 1)
                            dve.wait_ge(qsplit_done, 1)
                            link(nc.vector.tensor_tensor(qrest, qs[:, :], qpart[0], ALU.subtract))
                            nc.vector.tensor_copy(qpart[1], qrest).then_inc(qsplit_done, 1)
                            dve.wait_ge(qsplit_done, 2)
                            nc.vector.tensor_tensor(qpart[2], qrest, qpart[1], ALU.subtract).then_inc(qsplit_done, 1)
                            nc.vector.scalar_tensor_tensor(out=qabs[:, :], in0=qs[:, :], scalar=-1.0, in1=qs[:, :],
                                                           op0=ALU.mult, op1=ALU.max).then_inc(qabs_done, 1)
                    elif kind == "v":
                        c0, c1 = 4 * i, min(4 * i + 4, NCH)
                        k = KEYS[c1 - 1]
                        w = c1 - c0
                        bvv = bv_all[0:k, :].rearrange("p (h d) -> p h d", d=HD)
                        bvv = bass.AP(bvv.tensor, bvv.offset, [list(bvv.ap[0]), [0, w]] + [list(d) for d in bvv.ap[1:]])
                        nc.vector.tensor_tensor(vals[0:k, c0:c1, :, 0:HD],
                                                misc[0:k, 0:w * D].rearrange("p (c h d) -> p c h d", c=w, d=HD),
                                                bvv, ALU.add).then_inc(dve_took, 1)
                    elif kind == "shift":
                        if b > 0:
                            dve.wait_ge(shift_in, 16 * PARTS * b)
                        if exact:
                            nc.vector.memset(shift[:, :], 0.0).then_inc(dve_took, 1)
                        else:
                            nc.vector.tensor_copy(shift[:, :], misc[0:H, 0:S]).then_inc(dve_took, 1)
                        if b > 0:
                            return
                        dve.wait_ge(dve_took, by_vector[n])
                        link(nc.vector.tensor_copy(shift_part[0][:, :], shift[:, :]))
                        link(nc.vector.tensor_tensor(shift[:, :], shift[:, :], shift_part[0][:, :], ALU.subtract))
                        link(nc.vector.tensor_copy(shift_part[1][:, :], shift[:, :]))
                        nc.vector.tensor_tensor(shift_part[2][:, :], shift[:, :], shift_part[1][:, :],
                                                ALU.subtract).then_inc(shift_ready, 1)
                    elif kind == "simT":
                        nc.vector.tensor_copy(simT[:, :], misc[:, 0:E]).then_inc(dve_took, 1)
                    elif kind == "WpT":
                        nc.vector.tensor_copy(wg[:, 0:D], misc[:, 0:D]).then_inc(dve_took, 1)
                    elif kind == "WpSim":
                        nc.vector.tensor_copy(wg[:, D:GW], misc[:, 0:E]).then_inc(dve_took, 1)
                    elif kind == "oT":
                        o = misc[:, 0:S].rearrange("p (t r) -> p t r", r=32)
                        inv = inverses[:, b * HG + i]
                        flat_inv = inv.rearrange("p t j -> p (t j)")
                        link(nc.vector.tensor_scalar(flat_inv, o[:, :, HD], SUM_FLOOR, None, ALU.max))
                        link(nc.vector.reciprocal(flat_inv, flat_inv))
                        if i == 0 and b > 0:
                            dve.wait_ge(misc_full, number["onT", b - 1, 0] + 1)
                        r = bass.AP(inv.tensor, inv.offset, [list(d) for d in inv.ap] + [[0, HD]])
                        nc.vector.tensor_tensor(onat[:, :, 4 * i:4 * i + 4, :],
                                                misc[:, 0:S].rearrange("p (t j r) -> p t j r", t=TT, r=32)[:, :, :, 0:HD],
                                                r, ALU.mult).then_inc(dve_took, 1)
                    elif kind == "wo":
                        at = slice(b * TT, (b + 1) * TT)
                        if b == 0:
                            dve.wait_ge(bo_added, 1)
                        nc.vector.tensor_tensor(xs[:, at, :], xs[:, at, :],
                                                misc[:, 0:TT * D].rearrange("p (t d) -> p t d", t=TT),
                                                ALU.add).then_inc(dve_took, 1)
                        dve.wait_ge(dve_took, by_vector[n])
                        for t in range(TT):
                            moments_of(xs[:, b * TT + t, :], t)
                        nc.vector.tensor_scalar(var_eps[:, 0:TT], moments[:, 0:TT, 1], LN_EPS, None,
                                                ALU.add).then_inc(ve_ready, 1)
                    elif kind == "xnT":
                        nc.vector.tensor_copy(xn2T[:, :], misc[:, 0:S]).then_inc(dve_took, 1)
                    elif kind == "gate":
                        dve.wait_ge(sq_done, TT * (b + 1))
                        nc.vector.tensor_copy(graw[:, :, :], misc[:, 0:TT * GW].rearrange(
                            "p (t g) -> p t g", t=TT)[:, :, D:GW]).then_inc(dve_took, 1)
                        nc.vector.tensor_scalar(sumsq[:, :], sumsq[:, :], L2_EPS ** 2, None, ALU.max).then_inc(sq_pool, 1)
                    elif kind == "combT":
                        nc.vector.tensor_copy(combT[:, :], misc[0:E, 0:S]).then_inc(dve_took, 1)
                    elif kind == "b2":
                        at = slice(b * TT, (b + 1) * TT)
                        so_far = b * DOWNS if b == B - 1 else b * DOWNS + downs_before_b2
                        if so_far > 0:
                            dve.wait_ge(down_taken, so_far)
                        nc.vector.tensor_tensor(xs[:, at, :], xs[:, at, :],
                                                misc[:, 0:TT * D].rearrange("p (t d) -> p t d", t=TT),
                                                ALU.add).then_inc(dve_took, 1)

                def normalise(b):
                    dve.wait_ge(rstd_ready, b + 2)
                    for t in range(TT):
                        last = nc.vector.tensor_scalar(xn2[:, t, :], xs[:, b * TT + t, :], moments[:, t, 0:1],
                                                       rstd[:, t:t + 1], ALU.subtract, ALU.mult)
                        if t < TT - 1:
                            link(last)
                    last.then_inc(xn2_ready, 1)

                def choose(b, t):
                    if t == 0:
                        dve.wait_ge(rnorm_ready, b + 1)
                    link(nc.vector.tensor_scalar(gsc[:, t, :], graw[:, t, :], rnorm[:, t:t + 1], tiny[:, 1:2],
                                                 ALU.mult, ALU.mult))
                    link(nc.vector.max(top[:, t, :], gsc[:, t, :]))
                    link(nc.vector.max_index(topi[:, t, :], top[:, t, :], gsc[:, t, :]))
                    if t == TT - 1:
                        link(nc.vector.tensor_copy(topf[:, :, :], topi[:, :, :]))
                        nc.vector.tensor_tensor(diff[:, :], top[:, :, 1], top[:, :, 0],
                                                ALU.subtract).then_inc(diff_ready, 1)

                def combine(b):
                    dve.wait_ge(ediff_ready, b + 1)
                    link(nc.vector.tensor_scalar(den[:, :], ediff[:, :], 1.0, None, ALU.add))
                    link(nc.vector.reciprocal(p1[:, :], den[:, :]))
                    link(nc.vector.tensor_tensor(p2[:, :], ediff[:, :], p1[:, :], ALU.mult))
                    for t in range(TT):
                        link(nc.vector.tensor_scalar(hot[:, :], iota8[:, :], topf[:, t, 0:1], p1[:, t:t + 1],
                                                     ALU.is_equal, ALU.mult))
                        link(nc.vector.tensor_scalar(comb[:, t, :], iota8[:, :], topf[:, t, 1:2], p2[:, t:t + 1],
                                                     ALU.is_equal, ALU.mult))
                        link(nc.vector.tensor_tensor(comb[:, t, :], comb[:, t, :], hot[:, :], ALU.add))
                    dve.sem_inc(comb_ready, 1)

                def norm_sim():
                    link(nc.vector.reciprocal(tiny[:, 1:2], tiny[:, 0:1]))
                    link(nc.vector.tensor_tensor(junk[0:E, :], sim_rows[:, :], sim_rows[:, :], ALU.mult))
                    link(nc.vector.tensor_reduce(tiny[0:E, 4:5], junk[0:E, :], AX_X, ALU.add))
                    nc.vector.tensor_scalar(tiny[0:E, 2:3], tiny[0:E, 4:5], L2_EPS ** 2, None,
                                            ALU.max).then_inc(sq_pool, 1)

                def scale_sim():
                    dve.wait_ge(rsim_ready, 1)
                    nc.vector.tensor_scalar(sim_rows[:, :], sim_rows[:, :], tiny[0:E, 3:4], None,
                                            ALU.mult).then_inc(sn_ready, 1)

                def masked_scores(scores, buffer, ch):
                    k = KEYS[ch]
                    m = maskT[0:k, ch, :]
                    m4 = bass.AP(m.tensor, m.offset, [list(m.ap[0]), [0, 4], list(m.ap[1])])
                    return nc.vector.tensor_tensor(masked[0:k, buffer, :].rearrange("p (h s) -> p h s", h=4),
                                                   scores[0:k, :].rearrange("p (h s) -> p h s", h=4), m4, ALU.add)

                def judge():
                    flat_inv = inverses[:, :, :, :].rearrange("p g t j -> p (g t j)")
                    link(nc.vector.tensor_scalar(junk[:, 0:B * HG * TT * 4], flat_inv, 1.0 / SUM_LEAST, None, ALU.is_lt))
                    link(nc.vector.tensor_scalar(flat_inv, flat_inv, 1.0 / SUM_MOST, None, ALU.is_gt))
                    link(nc.vector.tensor_tensor(flat_inv, flat_inv, junk[:, 0:B * HG * TT * 4], ALU.min))
                    nc.vector.tensor_reduce(fine[:, 0:1], flat_inv, AX_X, ALU.min).then_inc(fine_ready, 1)

                def add_mask(g):
                    b, ch = g // SLOTS, g % NCH
                    k = KEYS[ch]
                    dve.wait_ge(scored, g + 1)
                    if g % SLOTS < NCH:
                        dve.wait_ge(act_took, by_scalar[number["maskT", b, ch // 2]])
                    if g >= NB:
                        dve.wait_ge(exp_done, g - NB + 1)
                    last = masked_scores(score[g % 2], g % NB, ch)
                    if exact:
                        link(last)
                        last = nc.vector.tensor_tensor(masked[0:k, g % NB, :], masked[0:k, g % NB, :], top_rows[0:k, :],
                                                       ALU.subtract)
                    last.then_inc(masked_done, 1)

                def largest(b, hg):
                    hgn = b * HG + hg
                    if hg == 0:
                        dve.wait_ge(act_took, by_scalar[number["maskT", b, NM2 - 1]])
                    if hgn > 0:
                        dve.wait_ge(exp_done, hgn * NCH)
                    for ch in range(NCH):
                        n = hgn * NCH + ch
                        k = KEYS[ch]
                        dve.wait_ge(top_scored, n + 1)
                        masked_scores(score[0], 0, ch).then_inc(top_masked, 1)
                        dve.wait_ge(top_turned, n + 1)
                        turned = score[1][:, :].rearrange("p (j k) -> p j k", k=P)[:, :, 0:k]
                        link(nc.vector.tensor_reduce(top_score[:, min(ch, 1), :], turned, AX_X, ALU.max))
                        if ch > 0:
                            link(nc.vector.tensor_tensor(top_score[:, 0, :], top_score[:, 0, :], top_score[:, 1, :],
                                                         ALU.max))
                        dve.sem_inc(top_reduced, 1)
                    tops = top_score[:, 0, :]
                    nc.vector.tensor_copy(masked[:, 0, :].rearrange("p (j k) -> p j k", k=P),
                                          bass.AP(tops.tensor, tops.offset, [list(d) for d in tops.ap] + [[0, P]])
                                          ).then_inc(top_spread, 1)
                    dve.wait_ge(top_back, hgn + 1)
                    link(nc.vector.tensor_copy(top_rows, score[1][:, :]))
                    dve.sem_inc(top_taken, 1)

                def take_values(hgn):
                    dve.wait_ge(pv_done, (hgn + 1) * NCH)
                    if hgn > 0:
                        dve.wait_ge(misc_full, number["oT", (hgn - 1) // HG, (hgn - 1) % HG] + 1)
                    nc.vector.tensor_copy(osum[:, :], pv[:, 0:S]).then_inc(pv_taken, 1)

                def hidden(b, unit):
                    _, h, e, part = unit
                    wait_for_pre(dve, b, unit)
                    k = (h * HALF + e) * FC + 2 * part
                    bias = bias_cols[:, k:k + 2]
                    bias = bass.AP(bias.tensor, bias.offset, [list(d) for d in bias.ap] + [[0, S]])
                    nc.vector.tensor_tensor(hid[:, e * FC + 2 * part:e * FC + 2 * part + 2, :],
                                            ffn[(b * UNITS + place[unit]) % 2][:, :].rearrange(
                                                "p (c s) -> p c s", c=2), bias, ALU.add).then_inc(pre_dve, 1)

                def take_down(b, unit):
                    _, h, e, t = unit
                    n = b * UNITS + place[unit]
                    dve.wait_ge(ffn_full, n + 1)
                    taken = read_count(b, unit) - 1
                    if b == B - 1 or taken >= b * DOWNS + downs_before_b2:
                        dve.wait_ge(dve_took, by_vector[number["b2", b, 0]])
                    if taken > 0:
                        dve.wait_ge(down_taken, taken)
                    n2 = b * TT + t
                    g_e = h * HALF + e
                    nc.vector.scalar_tensor_tensor(out=xs[:, n2, :], in0=ffn[n % 2][:, 0:D],
                                                   scalar=comb[:, t, g_e:g_e + 1], in1=xs[:, n2, :],
                                                   op0=ALU.mult, op1=ALU.add).then_inc(down_taken, 1)

                def take_unit(b, unit):
                    if reader[place[unit]] == "down":
                        take_down(b, unit)
                    elif reader[place[unit]] == "pre_dve":
                        hidden(b, unit)
                    if unit == order[-1]:
                        dve.wait_ge(down_taken, (b + 1) * DOWNS)
                        dve.sem_inc(result_ready, 1)

                link(nc.vector.memset(vals[:, :, :, HD:HD + 1], 1.0))
                nc.vector.memset(pv[:, :], 0.0).then_inc(zeroed, 1)
                dve.wait_ge(x_in, 16)
                for n in range(NT):
                    nc.vector.bn_stats(stats[:, n, :], xs[:, n, :]).then_inc(dve_step, 1)
                chain[0] += NT
                for n in range(NT):
                    dve.wait_ge(dve_step, chain[0] - NT + n + 1)
                    nc.vector.bn_aggr(moments[:, n, :], stats[:, n, :]).then_inc(dve_step, 1)
                chain[0] += NT
                dve.wait_ge(dve_step, chain[0])
                nc.vector.tensor_scalar(var_eps[:, :], moments[:, :, 1], LN_EPS, None, ALU.add).then_inc(ve_ready, 1)
                misc_step(0, *steps[0])
                dve.wait_ge(consts, 3)
                link(nc.vector.tensor_scalar(negblk[:, :], blk[:, :], -1.0, None, ALU.mult))
                for a in range(2):
                    link(nc.vector.tensor_reduce(half[:, a:a + 1], blk[:, :].rearrange("p (h a) -> p a h", a=2)[:, a, :],
                                                 AX_X, ALU.add))
                dve.wait_ge(rstd_ready, 1)
                for n in range(NT):
                    nc.vector.tensor_scalar(xn1[:, n * D:(n + 1) * D], xs[:, n, :], moments[:, n, 0:1],
                                            rstd[:, n:n + 1], ALU.subtract, ALU.mult).then_inc(xn1_ready, 1)
                for n, (kind, b, i) in enumerate(before):
                    if kind == "shift":
                        key_extremes(0)
                        split_keys_first()
                    if kind == "v" and i == 0:
                        dve.wait_ge(w_in, 16 * 8)
                    if n > 0:
                        misc_step(n, kind, b, i)
                dve.wait_ge(consts, 4)
                for b in range(B):
                    for slot in range(SLOTS):
                        g = b * SLOTS + slot
                        if slot % NCH == LAG and g > LAG:
                            take_values(g // NCH - 1)
                        for step in at_slot[b, slot]:
                            misc_step(*step)
                        if exact and slot % NCH == 0:
                            largest(b, slot // NCH)
                        add_mask(g)
                        if b == 0 and slot == 12:
                            norm_sim()
                        if b == 0 and slot == 25:
                            scale_sim()
                        if b + 1 < B and slot == KEYS_SLOT:
                            key_extremes(b + 1)
                        if b + 1 < B and slot == BOUND_SLOT:
                            bound(b + 1)
                        if b > 0:
                            if slot == NORM_SLOT:
                                normalise(b - 1)
                            if slot in CHOOSE_SLOTS:
                                choose(b - 1, CHOOSE_SLOTS.index(slot))
                            if slot == COMBINE_SLOT:
                                combine(b - 1)
                        for fb, unit in units_in(b, slot):
                            take_unit(fb, unit)
                take_values(B * HG - 1)
                for n in range(first_after, len(steps) - 1):
                    if steps[n][0] == "xnT":
                        normalise(B - 1)
                    if steps[n][0] == "combT":
                        between = [lambda: choose(B - 1, 0), lambda: choose(B - 1, 1), lambda: combine(B - 1)]
                        for unit in first_half:
                            take_unit(B - 1, unit)
                            if unit[3] == 0 and unit[2] < len(between):
                                between[unit[2]]()
                    misc_step(n, *steps[n])
                    for unit in late_at.get(steps[n][0], []):
                        take_unit(B - 2, unit)
                for unit in mixed + last_half:
                    take_unit(B - 1, unit)
                judge()
                misc_step(len(steps) - 1, *steps[-1])

        with ExitStack() as own:
            attempt(own, False)
        redo = nc.values_load(verdict[0:1, 0:1], min_val=0, max_val=1)
        with nc.If(redo != 0):
            with ExitStack() as own:
                attempt(own, True)


_INS = ["x", "ctx_1024", "mask_Bx1xSxS2_ff0", "L0_xattn_Wq", "L0_xattn_bq", "L0_xattn_Wk", "L0_xattn_bk",
        "L0_xattn_Wv", "L0_xattn_bv", "L0_xattn_Wo", "L0_xattn_bo", "L0_ffn_Wp", "L0_ffn_sim_matrix",
        "L0_ffn_temperature", "L0_ffn_W1", "L0_ffn_b1", "L0_ffn_W2", "L0_ffn_b2"]


def kernel(**inputs):
    import numpy as _np
    import concourse.bacc as _bacc
    from concourse import mybir as _mybir
    from concourse.bass_utils import run_bass_kernel_spmd as _run

    nc = _bacc.Bacc("TRN2", target_bir_lowering=False, num_devices=1)
    arrays, args = {}, []
    for name in _INS:
        a = _np.ascontiguousarray(inputs[name])
        if a.ndim == 0:
            a = a.reshape(1)
        arrays[f"in_{name}_dram"] = a
        args.append(nc.dram_tensor(f"in_{name}_dram", a.shape, _mybir.dt.from_np(a.dtype), kind="ExternalInput").ap())
    shape = inputs["x"].shape
    args.append(nc.dram_tensor("out_0_dram", shape, _mybir.dt.float32, kind="ExternalOutput").ap())
    layer(nc, *args)
    r = _run(nc, [arrays], core_ids=[0])
    return r.results[0]["out_0_dram"]
```
